# Optimizing a Trainium2 kernel written in Bass

```python
import numpy as np
import jax
import jax.numpy as jnp

def _softmax(x, axis=-1):
    return jax.nn.softmax(x, axis=axis)

def _gelu(x):
    return jax.nn.gelu(x, approximate=True)

def _silu(x):
    return jax.nn.silu(x)

def _sigmoid(x):
    return jax.nn.sigmoid(x)

def _layernorm(x, axis=-1, eps=1e-05):
    m = jnp.mean(x, axis=axis, keepdims=True)
    v = jnp.var(x, axis=axis, keepdims=True)
    return (x - m) / jnp.sqrt(v + eps)

def _scatter_add(tgt, idx, src, axis=0):
    return tgt.at[idx].add(src)

def _segment_sum(src, seg, n):
    return jax.ops.segment_sum(src, seg, n)
kernel_name = 'mk_xattn_ffn_d1_seqx_r4_1aa149'

def setup_inputs(seed: int=0):
    np.random.seed(seed)
    _w = jnp.asarray

    def _rec_inputs():
        import jax
        import jax.numpy as jnp
        _rk = jax.random.key(seed)
        x = -0.000125 + 0.9999 * jax.random.normal(jax.random.fold_in(_rk, 1), (16, 100, 512), jnp.float32)
        _lenS = 100 - jax.random.randint(jax.random.fold_in(_rk, 7), (16,), 0, max(1, 100 // 4) + 1, jnp.int32)
        _lenS2 = 361 - jax.random.randint(jax.random.fold_in(_rk, 8), (16,), 0, max(1, 361 // 4) + 1, jnp.int32)
        _ctx_2048P = jax.random.normal(jax.random.fold_in(_rk, 11), (16, 16, 512), jnp.float32)
        _ctx_2048c = jax.random.dirichlet(jax.random.fold_in(_rk, 511), 0.3 * jnp.ones((16,), jnp.float32), (16, 361))
        _ctx_2048t = jnp.einsum('bsk,bkd->bsd', _ctx_2048c, _ctx_2048P)
        _ctx_2048t = _ctx_2048t * jax.lax.rsqrt(jnp.mean(jnp.square(_ctx_2048t)) + 1e-12) * 0.953939
        ctx_2048 = -0.000514642 + 1.00011 * (_ctx_2048t + 0.3 * jax.random.normal(jax.random.fold_in(_rk, 611), (16, 361, 512), jnp.float32))
        _validS = jnp.arange(100)[None, :] < _lenS[:, None]
        _validS2 = jnp.arange(361)[None, :] < _lenS2[:, None]
        _causal = jnp.tril(jnp.ones((100, 100), dtype=bool))
        mask_BxS2_bk0 = jnp.logical_not(jnp.broadcast_to(_validS2[:, :], (16, 361)))
        return (x, ctx_2048, mask_BxS2_bk0)
    x, ctx_2048, mask_BxS2_bk0 = _rec_inputs()

    def _L0_xattn_setup():
        import jax, jax.numpy as jnp
        import numpy as np
        H = 512
        NH = 16
        HD = H // NH
        EPS = 1e-06

        def rmsnorm(x, w, eps=EPS):
            var = jnp.mean(x * x, axis=-1, keepdims=True)
            return x * jax.lax.rsqrt(var + eps) * w
        key = jax.random.key(seed)
        ks = jax.random.split(key, 9)
        B, L, M = (4, 1024, 64)
        s = 1.0 / np.sqrt(H)
        return {'hidden_states': jax.random.normal(ks[0], (B, L, H), dtype=jnp.float32), 'memory_tokens': jax.random.normal(ks[1], (B, M, H), dtype=jnp.float32), 'memory_mask': jax.random.randint(ks[2], (B, M), 0, 2).astype(bool), 'norm_w': jnp.ones((H,), dtype=jnp.float32), 'wq': jax.random.normal(ks[3], (H, H), dtype=jnp.float32) * s, 'wk': jax.random.normal(ks[4], (H, H), dtype=jnp.float32) * s, 'wv': jax.random.normal(ks[5], (H, H), dtype=jnp.float32) * s, 'wo': jax.random.normal(ks[6], (H, H), dtype=jnp.float32) * s, 'wg': jax.random.normal(ks[7], (H, H), dtype=jnp.float32) * s}
    _L0_xattn_all = _L0_xattn_setup()
    _L0_xattn_in = {k: v for k, v in _L0_xattn_all.items() if k in ('norm_w', 'wq', 'wk', 'wv', 'wo', 'wg')}
    del _L0_xattn_all

    def _L0_ffn_setup():
        import jax, jax.numpy as jnp
        import numpy as np
        EPS = 1e-06
        K_STEPS = 4
        USE_GATING = True

        def layer_norm(x, gamma, beta):
            mu = jnp.mean(x, axis=-1, keepdims=True)
            var = jnp.mean(jnp.square(x - mu), axis=-1, keepdims=True)
            return (x - mu) * jax.lax.rsqrt(var + EPS) * gamma + beta
        key = jax.random.key(seed)
        B, L, D, H = (4, 1024, 512, 2048)
        ks = jax.random.split(key, 16)
        s = 0.02
        return {'x': jax.random.normal(ks[0], (B, L, D), dtype=jnp.float32), 'in_gamma': jnp.ones((D,), jnp.float32), 'in_beta': jnp.zeros((D,), jnp.float32), 'agg_w': jax.random.normal(ks[1], (D, D), jnp.float32) * s, 'agg_b': jnp.zeros((D,), jnp.float32), 'pn_gamma': jnp.ones((D,), jnp.float32), 'pn_beta': jnp.zeros((D,), jnp.float32), 'd1_w': jax.random.normal(ks[2], (D, H), jnp.float32) * s, 'd1_b': jnp.zeros((H,), jnp.float32), 'd2_w': jax.random.normal(ks[3], (H, D), jnp.float32) * s, 'd2_b': jnp.zeros((D,), jnp.float32), 'bc_w': jax.random.normal(ks[4], (D, D), jnp.float32) * s, 'bc_b': jnp.zeros((D,), jnp.float32), 'gate_w': jax.random.normal(ks[5], (D, D), jnp.float32) * s, 'gate_b': jnp.zeros((D,), jnp.float32), 'out_gamma': jnp.ones((D,), jnp.float32), 'out_beta': jnp.zeros((D,), jnp.float32)}
    _L0_ffn_all = _L0_ffn_setup()
    _L0_ffn_in = {k: v for k, v in _L0_ffn_all.items() if k in ('in_gamma', 'in_beta', 'agg_w', 'agg_b', 'pn_gamma', 'pn_beta', 'd1_w', 'd1_b', 'd2_w', 'd2_b', 'bc_w', 'bc_b', 'gate_w', 'gate_b', 'out_gamma', 'out_beta')}
    del _L0_ffn_all
    return {'x': x, 'ctx_2048': ctx_2048, 'mask_BxS2_bk0': mask_BxS2_bk0, 'L0_xattn_norm_w': _L0_xattn_in['norm_w'], 'L0_xattn_wq': _L0_xattn_in['wq'], 'L0_xattn_wk': _L0_xattn_in['wk'], 'L0_xattn_wv': _L0_xattn_in['wv'], 'L0_xattn_wo': _L0_xattn_in['wo'], 'L0_xattn_wg': _L0_xattn_in['wg'], 'L0_ffn_in_gamma': _L0_ffn_in['in_gamma'], 'L0_ffn_in_beta': _L0_ffn_in['in_beta'], 'L0_ffn_agg_w': _L0_ffn_in['agg_w'], 'L0_ffn_agg_b': _L0_ffn_in['agg_b'], 'L0_ffn_pn_gamma': _L0_ffn_in['pn_gamma'], 'L0_ffn_pn_beta': _L0_ffn_in['pn_beta'], 'L0_ffn_d1_w': _L0_ffn_in['d1_w'], 'L0_ffn_d1_b': _L0_ffn_in['d1_b'], 'L0_ffn_d2_w': _L0_ffn_in['d2_w'], 'L0_ffn_d2_b': _L0_ffn_in['d2_b'], 'L0_ffn_bc_w': _L0_ffn_in['bc_w'], 'L0_ffn_bc_b': _L0_ffn_in['bc_b'], 'L0_ffn_gate_w': _L0_ffn_in['gate_w'], 'L0_ffn_gate_b': _L0_ffn_in['gate_b'], 'L0_ffn_out_gamma': _L0_ffn_in['out_gamma'], 'L0_ffn_out_beta': _L0_ffn_in['out_beta']}

def reference(x, ctx_2048, mask_BxS2_bk0, L0_xattn_norm_w, L0_xattn_wq, L0_xattn_wk, L0_xattn_wv, L0_xattn_wo, L0_xattn_wg, L0_ffn_in_gamma, L0_ffn_in_beta, L0_ffn_agg_w, L0_ffn_agg_b, L0_ffn_pn_gamma, L0_ffn_pn_beta, L0_ffn_d1_w, L0_ffn_d1_b, L0_ffn_d2_w, L0_ffn_d2_b, L0_ffn_bc_w, L0_ffn_bc_b, L0_ffn_gate_w, L0_ffn_gate_b, L0_ffn_out_gamma, L0_ffn_out_beta):
    import jax
    import jax.numpy as jnp

    def _L0_xattn_ref(hidden_states, memory_tokens, memory_mask, norm_w, wq, wk, wv, wo, wg):
        import jax, jax.numpy as jnp
        import numpy as np
        H = 512
        NH = 16
        HD = H // NH
        EPS = 1e-06

        def rmsnorm(x, w, eps=EPS):
            var = jnp.mean(x * x, axis=-1, keepdims=True)
            return x * jax.lax.rsqrt(var + eps) * w
        B, L, C = hidden_states.shape
        M = memory_tokens.shape[1]
        scale = HD ** (-0.5)
        x = rmsnorm(hidden_states, norm_w)
        q = (x @ wq.T).reshape(B, L, NH, HD)
        k = (memory_tokens @ wk.T).reshape(B, M, NH, HD)
        v = (memory_tokens @ wv.T).reshape(B, M, NH, HD)
        attn = jnp.einsum('blhd,bmhd->bhlm', q, k) * scale
        attn = jnp.where(memory_mask[:, None, None, :], attn, -jnp.inf)
        attn = jax.nn.softmax(attn, axis=-1)
        attn = jnp.nan_to_num(attn, nan=0.0)
        out = jnp.einsum('bhlm,bmhd->blhd', attn, v).reshape(B, L, C)
        out = out @ wo.T
        gate = jax.nn.sigmoid(x @ wg.T)
        return gate * out

    def _L0_ffn_ref(x, in_gamma, in_beta, agg_w, agg_b, pn_gamma, pn_beta, d1_w, d1_b, d2_w, d2_b, bc_w, bc_b, gate_w, gate_b, out_gamma, out_beta):
        import jax, jax.numpy as jnp
        import numpy as np
        EPS = 1e-06
        K_STEPS = 4
        USE_GATING = True

        def layer_norm(x, gamma, beta):
            mu = jnp.mean(x, axis=-1, keepdims=True)
            var = jnp.mean(jnp.square(x - mu), axis=-1, keepdims=True)
            return (x - mu) * jax.lax.rsqrt(var + EPS) * gamma + beta
        x_norm = layer_norm(x, in_gamma, in_beta)
        thought = x_norm[:, -1, :] @ agg_w + agg_b
        for _ in range(K_STEPS):
            t = layer_norm(thought, pn_gamma, pn_beta)
            t = jax.nn.gelu(t @ d1_w + d1_b, approximate=False)
            thought = thought + (t @ d2_w + d2_b)
        broadcast = (thought @ bc_w + bc_b)[:, None, :]
        if USE_GATING:
            gate = jax.nn.sigmoid(x @ gate_w + gate_b)
            out = x + gate * broadcast
        else:
            out = x + broadcast
        return layer_norm(out, out_gamma, out_beta)
    x = x + _L0_xattn_ref(_layernorm(x, axis=-1), ctx_2048, mask_BxS2_bk0, L0_xattn_norm_w, L0_xattn_wq, L0_xattn_wk, L0_xattn_wv, L0_xattn_wo, L0_xattn_wg)
    x = x + _L0_ffn_ref(_layernorm(x, axis=-1), L0_ffn_in_gamma, L0_ffn_in_beta, L0_ffn_agg_w, L0_ffn_agg_b, L0_ffn_pn_gamma, L0_ffn_pn_beta, L0_ffn_d1_w, L0_ffn_d1_b, L0_ffn_d2_w, L0_ffn_d2_b, L0_ffn_bc_w, L0_ffn_bc_b, L0_ffn_gate_w, L0_ffn_gate_b, L0_ffn_out_gamma, L0_ffn_out_beta)
    return x

_drawn_inputs = setup_inputs


def setup_inputs(seed=0):
    import zlib

    import numpy as np

    out = dict(_drawn_inputs(seed))
    spreads = {'L0_xattn_norm_w': (1.0, 0.2),
     'L0_ffn_in_gamma': (1.0, 0.6),
     'L0_ffn_in_beta': (0.0, 0.739),
     'L0_ffn_agg_b': (0.0, 0.371),
     'L0_ffn_pn_gamma': (1.0, 0.6),
     'L0_ffn_pn_beta': (0.0, 0.662),
     'L0_ffn_d1_b': (0.0, 0.319),
     'L0_ffn_d2_b': (0.0, 0.1),
     'L0_ffn_bc_b': (0.0, 0.342),
     'L0_ffn_gate_b': (0.0, 0.8),
     'L0_ffn_out_gamma': (1.0, 0.2),
     'L0_ffn_out_beta': (0.0, 0.1)}
    factors = {}
    for name, (base, spread) in spreads.items():
        noise = np.random.default_rng([zlib.crc32(name.encode()), seed]).standard_normal(out[name].shape)
        drawn = base * np.exp(spread * noise) if base else spread * noise
        out[name] = jnp.asarray(drawn.astype(out[name].dtype))
    for name, factor in factors.items():
        out[name] = (out[name] * factor).astype(out[name].dtype)
    return out
```

```python
from contextlib import ExitStack

import concourse.bass as bass
from concourse import mybir

F32 = mybir.dt.float32
BF16 = mybir.dt.bfloat16
I32 = mybir.dt.int32
ALU = mybir.AluOpType
ACT = mybir.ActivationFunctionType
AX_X = mybir.AxisListType.X

B, L, D, M = 16, 100, 512, 361
NH, HD = 16, 32
P = 128
KD = D // P
GB = 4
NG = B // GB
GL = GB * L
F = 2048
FJ = F // D
FS = F // P
STEPS = 4
TAIL = M // 4
HEAD_ROWS = M - TAIL
SCALE = float(HD) ** -0.5
EPS_LN, EPS_IN = 1e-5, 1e-6
MASKED = -1e30
ALIVE = -5e29


class Geometry:

    def __init__(self, full):
        self.full = full
        self.keys = M if full else TAIL
        self.bank_heads = 1 if full else KD
        self.unit_heads = 2 * self.bank_heads
        self.units = 8
        self.lots = GB if full else 1
        self.group_units = self.units * self.lots
        self.lot_keys = self.keys * (1 if full else GB)
        self.chunks = [(c, min(P, self.keys - c)) for c in range(0, self.keys, P)]
        self.v_tiles = len(self.chunks) if full else GB

    def batch(self, lot, u):
        return lot if self.full else u // 2

    def heads(self, u, k):
        if self.full:
            return [2 * u + k]
        first = 8 * (u % 2) + 4 * k
        return list(range(first, first + 4))


def xattn_ffn(nc, a):
    ctx = ExitStack()
    with ctx:
        def sb(name, shape, dt=F32):
            return ctx.enter_context(nc.sbuf_tensor(name, shape, dt))

        def sem(name):
            return ctx.enter_context(nc.semaphore(name))

        x = sb("x", [L, B, D])
        w_arena = sb("w_arena", [P, 4 * KD * D])
        kv_arena = sb("kv_arena", [P, FS * D])
        t_arena = sb("t_arena", [P, KD * B * L])
        c_arena = sb("c_arena", [P, 3200])
        wo = sb("wo", [P, KD, D])
        fg = sb("fg", [P, KD, D])
        agg = sb("agg", [P, KD, D])
        bc = sb("bc", [P, KD, D])
        probs_t = sb("probs_t", [P, 800])
        normed = sb("normed", [L, 2, D])
        gamma_row = sb("gamma_row", [L, D])
        beta_row = sb("beta_row", [L, D])
        mask_bias = sb("mask_bias", [1, B * M], BF16)
        mask_any = sb("mask_any", [B, HEAD_ROWS], mybir.dt.uint8)
        flag_a = sb("flag_a", [32, 32])
        flag_b = sb("flag_b", [32, 32])
        flag = sb("flag", [1, 4], I32)
        ident = sb("ident", [P, P])
        pick = sb("pick", [P, B])
        ones_bf = sb("ones_bf", [1, P], BF16)
        ones = sb("ones", [1, B])
        minus_half = sb("minus_half", [L, B])
        vecs = sb("vecs", [P, 5, KD])
        pn_vecs = sb("pn_vecs", [P, 2, KD])
        d1b = sb("d1b", [P, KD, FJ])
        agg_b = sb("agg_b", [1, D])
        d2_b = sb("d2_b", [1, D])
        half_gate_b = sb("half_gate_b", [P, KD])
        st = sb("st", [L, GB, 6])
        mv = sb("mv", [L, GB, 2])
        vr = sb("vr", [L, GB])
        rstd = sb("rstd", [L, GB])
        st1 = sb("st1", [L, GB, 6])
        mv1 = sb("mv1", [L, GB, 2])
        mean1 = sb("mean1", [L, B])
        vr1 = sb("vr1", [L, B])
        rstd1 = sb("rstd1", [L, B])
        row_max = sb("row_max", [L, 2, 8])
        row_sum = sb("row_sum", [L, 2, 8])
        row_inv = sb("row_inv", [L, 2, 8])
        last_row = sb("last_row", [B, D])
        thought = sb("thought", [B, D])
        th_norm = sb("th_norm", [B, D])
        th_st = sb("th_st", [B, 6])
        th_mv = sb("th_mv", [B, 2])
        th_var = sb("th_var", [B, 1])
        th_rstd = sb("th_rstd", [B, 1])
        th_t0 = sb("th_t0", [P, KD, B])
        th_t = sb("th_t", [P, KD, 32])
        hid_t = sb("hid_t", [P, FS, 32])
        bc_half = sb("bc_half", [P, KD, B])
        o_st = sb("o_st", [L, GB, 6])
        o_mv = sb("o_mv", [L, GB, 2])
        o_var = sb("o_var", [L, GB])
        o_rstd = sb("o_rstd", [L, GB])
        o_shift = sb("o_shift", [L, GB])

        wk, wv, wq, wg = (w_arena[:, i * KD * D:(i + 1) * KD * D].rearrange("p (k n) -> p k n", k=KD)
                          for i in range(4))
        d1 = w_arena[:, :].rearrange("p (k n) -> p k n", k=KD)
        KCOLS = NH * M
        keys = kv_arena[:, 0:KCOLS]
        values = kv_arena[:, KCOLS:KCOLS + GB * D].rearrange("p (c n) -> p c n", c=GB)
        d2 = kv_arena[:, :].rearrange("p (k n) -> p k n", k=FS)
        x_t, q_t, gate_t, att_t = (t_arena[:, i * KD * GL:(i + 1) * KD * GL].rearrange("p (k n) -> p k n", k=KD)
                                   for i in range(4))
        mask_row = att_t[0:1, :, :].rearrange("p k n -> p (k n)").bitcast(mybir.dt.uint8)
        gates = t_arena[:, :].rearrange("p (k n) -> p k n", k=KD)
        ctx_t = c_arena[:, 0:KD * M]
        UNIT = 722
        probs = [c_arena[0:L, KD * M + i * UNIT:KD * M + (i + 1) * UNIT] for i in range(2)]
        x2_t = c_arena[:, 0:KD * GL].rearrange("p (k n) -> p k n", k=KD)
        hid = parts = c_arena[:, 1600:1600 + D]
        z_t = c_arena[:, 1600 + D:1600 + D + FS * B]
        lift = c_arena[:, 0:2 * KD * L].rearrange("p (s k n) -> p s k n", s=2, k=KD)
        mixed = kv_arena[0:L, 0:GB * D].rearrange("p (s n) -> p s n", s=GB)
        final = kv_arena[0:L, GB * D:2 * GB * D].rearrange("p (s n) -> p s n", s=GB)
        norm_w, in_gamma, in_beta, gate_b, bc_b = (vecs[:, i, :] for i in range(5))
        pn_gamma, pn_beta = (pn_vecs[:, i, :] for i in range(2))

        ps_s = ctx.enter_context(nc.psum_tensor("ps_s", [P, 2, 512], F32))
        ps_pt = ctx.enter_context(nc.psum_tensor("ps_pt", [P, 2, 512], F32))
        ps_mm = [ctx.enter_context(nc.psum_tensor(f"ps_mm{i}", [P, 512], F32)) for i in range(2)]
        ps_pv = ctx.enter_context(nc.psum_tensor("ps_pv", [P, 512], F32))
        ps_tr = ctx.enter_context(nc.psum_tensor("ps_tr", [P, 512], F32))

        x_first_loaded, x_rest_loaded, ctx_loaded, const_loaded, mask_loaded, mask_row_loaded, row_loaded = (
            sem(n) for n in ("x_first_loaded", "x_rest_loaded", "ctx_loaded", "const_loaded", "mask_loaded",
                             "mask_row_loaded", "row_loaded"))
        w_loaded = {n: sem(f"{n}_loaded") for n in ("wq", "wk", "wg", "wv", "wo", "fg", "agg", "bc", "d1", "d2")}
        last_row_loaded = sem("last_row_loaded")
        stored = [sem(f"stored{s}") for s in range(GB)]
        filled, zeroed, bias_made, flag_step, flag_set, half_made = (
            sem(n) for n in ("filled", "zeroed", "bias_made", "flag_step", "flag_set", "half_made"))
        st_made, mv_made, var_ready, rstd_ready, norm_ready = (
            sem(n) for n in ("st_made", "mv_made", "var_ready", "rstd_ready", "norm_ready"))
        xt_done, xt_kept, back1_done = sem("xt_done"), sem("xt_kept"), sem("back1_done")
        done = {k: sem(f"{k}_done") for k in ("q", "k", "v", "g", "o")}
        kept = {k: sem(f"{k}_kept") for k in ("q", "k", "v", "g", "o")}
        scored, maxed, shifted, raised, summed, inverted, weighted, divided, turned, turn_kept, mixed_v, mix_kept = (
            sem(n) for n in ("scored", "maxed", "shifted", "raised", "summed", "inverted", "weighted", "divided",
                             "turned", "turn_kept", "mixed_v", "mix_kept"))
        x1_ready, st1_made, mv1_made, mean1_ready, var1_ready, rstd1_ready = (
            sem(n) for n in ("x1_ready", "st1_made", "mv1_made", "mean1_ready", "var1_ready", "rstd1_ready"))
        norm2_ready, tr2_done, tr2_used, fg_done, fg_kept = (
            sem(n) for n in ("norm2_ready", "tr2_done", "tr2_used", "fg_done", "fg_kept"))
        th_ready, th_st_made, th_mv_made, th_var_ready, th_rstd_ready, th_normed = (
            sem(n) for n in ("th_ready", "th_st_made", "th_mv_made", "th_var_ready", "th_rstd_ready", "th_normed"))
        (tht_done, tht_scaled, tht_ready, up_done, up_kept, upt_done, z_ready, hid_ready, down_done,
         down_kept, sum_done) = (sem(n) for n in (
             "tht_done", "tht_scaled", "tht_ready", "up_done", "up_kept", "upt_done", "z_ready",
             "hid_ready", "down_done", "down_kept", "sum_done"))
        agg_done, bc_done, bc_ready = sem("agg_done"), sem("bc_done"), sem("bc_ready")
        (lifted, back_done, o_ready, o_st_made, o_mv_made, o_var_ready, o_rstd_ready, o_shift_ready, o_normed,
         o_scaled, o_biased, out_ready) = (sem(n) for n in (
             "lifted", "back_done", "o_ready", "o_st_made", "o_mv_made", "o_var_ready", "o_rstd_ready",
             "o_shift_ready", "o_normed", "o_scaled", "o_biased", "out_ready"))

        tail, full = Geometry(False), Geometry(True)

        def each_group(eng, body):
            with eng.Fori(0, NG - 1) as g:
                body(g, False)
            body(NG - 1, True)

        def each_out(eng, body):
            for s in range(GB):
                body(0, s)
            with eng.Fori(1, NG - 1) as g:
                for s in range(GB):
                    body(g, s)
            for s in range(GB):
                body(NG - 1, s)

        passed = {"pe": sem("pe_passed"), "dve": sem("dve_passed")}

        def wait_apart(eng, signal, value):
            eng.wait_ge(signal, value)
            eng.sem_inc(passed["pe" if signal is th_normed else "dve"], 1)

        def branch(eng, tail_part, full_part):
            eng.wait_ge(flag_set, 1)
            seen = eng.value_load(flag[0:1, 0:1], min_val=0, max_val=1)
            with eng.If(seen > 0):
                full_part()
            with eng.Else():
                tail_part()

        block = ctx.enter_context(nc.Block())

        @block.sync
        def _(sp):
            def load_x(first, n, signal):
                sp.dma_start(x[:, first:first + n, :],
                             a["x"][first:first + n].rearrange("b l d -> l b d")).then_inc(signal, 16)

            def load_w(name, dst):
                sp.dma_start(dst, a[name]).then_inc(w_loaded[name], 16)

            def load_ctx(geo, i):
                src = a["ctx_full"] if geo.full else a["ctx_tail"]
                sp.dma_start(ctx_t[:, 0:KD * geo.lot_keys],
                             src[bass.ds(i, 1)].rearrange("a p n -> p (a n)")).then_inc(ctx_loaded, 16)

            def load_mask_row(geo):
                src = a["mask_row_full"] if geo.full else a["mask_row_tail"]
                sp.dma_start(mask_row[:, 0:B * geo.keys], src).then_inc(mask_row_loaded, 16)

            def load_rest():
                load_w("wv", wv)
                load_w("wg", wg)
                load_x(GB, B - GB, x_rest_loaded)
                load_w("wo", wo[:, :, :])
                load_w("agg", agg[:, :, :])
                load_w("fg", fg[:, :, :])
                load_w("bc", bc[:, :, :])
                for dst, name in ((pick, "pick"), (pn_vecs, "pn_vecs"), (d1b, "d1b"), (agg_b, "agg_b"),
                                  (d2_b, "d2_b")):
                    sp.dma_start(dst[:], a[name]).then_inc(row_loaded, 16)
                for dst, name in ((gamma_row, "out_gamma"), (beta_row, "out_beta")):
                    sp.dma_start(dst[:, :], a[name].to_broadcast([L, D])).then_inc(row_loaded, 16)

            sp.dma_start(mask_any[:, :], a["mask"][:, 0:HEAD_ROWS]).then_inc(mask_loaded, 16)
            sp.dma_start(ident[:, :], a["ident"]).then_inc(const_loaded, 16)
            load_x(0, GB, x_first_loaded)
            sp.dma_start(vecs[:, :, :], a["vecs"]).then_inc(const_loaded, 16)
            load_w("wq", wq)
            load_w("wk", wk)

            def attend(geo):
                load_mask_row(geo)
                load_ctx(geo, 0)
                load_rest()
                with sp.Fori(1, NG * geo.lots) as i:
                    sp.wait_ge(done["v"], geo.v_tiles * i)
                    load_ctx(geo, i)
                sp.wait_ge(done["v"], geo.v_tiles * NG * geo.lots)
                sp.wait_ge(done["g"], KD * NG)
                load_w("d1", d1)
                sp.wait_ge(mixed_v, geo.group_units * NG)
                load_w("d2", d2)

            branch(sp, lambda: attend(tail), lambda: attend(full))
            sp.wait_ge(x1_ready, B)
            sp.dma_start(last_row[:, :], x[L - 1:L, :, :]).then_inc(last_row_loaded, 16)
            with sp.Fori(0, NG) as g:
                for s in range(GB):
                    sp.wait_ge(out_ready, GB * g + s + 1)
                    sp.dma_start(a["out"][bass.ds(GB * g + s, 1)].rearrange("b l d -> l (b d)"),
                                 final[:, s, :]).then_inc(stored[s], 16)
            for s in range(GB):
                sp.wait_ge(stored[s], 16 * NG)

        @block.tensor
        def _(pe):
            mm_uses = []

            def project(kind, count, rows, cols, mats, need=()):
                use = len(mm_uses)
                bank = ps_mm[use % 2]
                if use >= 2:
                    kind2, count2 = mm_uses[use - 2]
                    pe.wait_ge(kept[kind2], count2)
                for s, v in need:
                    pe.wait_ge(s, v)
                for k in range(KD):
                    lhs, rhs = mats(k)
                    mm = pe.matmul(bank[0:rows, 0:cols], lhs, rhs, start=(k == 0), stop=(k == KD - 1))
                mm.then_inc(done[kind], 1)
                mm_uses.append((kind, count))

            def turn_x(n, b):
                if b:
                    pe.wait_ge(xt_kept, GB * n + b)
                pe.wait_ge(norm_ready, GB * n + b + 1)
                for k in range(KD):
                    t = pe.transpose(ps_tr[:, k * L:(k + 1) * L], normed[:, b % 2, k * P:(k + 1) * P],
                                     ident[0:L, 0:L])
                t.then_inc(xt_done, 1)

            def project_q(n, m):
                project("q", KD * n + m + 1, P, GL, lambda k: (wq[:, k, m * P:(m + 1) * P], x_t[:, k, :]),
                        [(w_loaded["wq"], 16), (xt_kept, GB * n + GB)])

            def project_g(n, m):
                project("g", KD * n + m + 1, P, GL, lambda k: (wg[:, k, m * P:(m + 1) * P], x_t[:, k, :]),
                        [(w_loaded["wg"], 16), (xt_kept, GB * n + GB)])

            def ctx_cols(geo, k):
                return ctx_t[:, k * geo.lot_keys:(k + 1) * geo.lot_keys]

            def project_k(geo, i, m):
                project("k", KD * i + m + 1, P, geo.lot_keys,
                        lambda k: (wk[:, k, m * P:(m + 1) * P], ctx_cols(geo, k)),
                        [(w_loaded["wk"], 16), (ctx_loaded, 16 * i + 16)])

            def project_v(geo, i, c):
                first, rows = geo.chunks[c] if geo.full else (c * TAIL, TAIL)
                project("v", geo.v_tiles * i + c + 1, rows, D,
                        lambda k: (ctx_cols(geo, k)[:, first:first + rows], wv[:, k, :]),
                        [(w_loaded["wv"], 16), (ctx_loaded, 16 * i + 16)])

            def project_o(g, m):
                project("o", KD * g + m + 1, P, GL, lambda k: (wo[:, k, m * P:(m + 1) * P], att_t[:, k, :]),
                        [(w_loaded["wo"], 16)])

            def scores(geo, g, lot, u):
                unit = geo.group_units * g + geo.units * lot + u
                i = geo.lots * g + lot
                b = geo.batch(lot, u)
                if u == 0:
                    pe.wait_ge(kept["q"], KD * g + KD)
                    pe.wait_ge(kept["k"], KD * i + KD)
                if u or lot:
                    pe.wait_ge(shifted, unit)
                w = geo.bank_heads * geo.keys
                for k in range(2):
                    h0 = geo.heads(u, k)[0]
                    col = (h0 if geo.full else NH * b + h0) * geo.keys
                    bank = ps_s[0:L, k, 0:w]
                    pe.matmul(bank, q_t[:, h0 // 4, b * L:(b + 1) * L], keys[:, col:col + w], start=True, stop=False)
                    bias = mask_bias[:, bass.ds((GB * g + b) * geo.keys, geo.keys)]
                    if geo.bank_heads > 1:
                        bias = bias.unsqueeze(1).to_broadcast([1, geo.bank_heads, geo.keys])
                    mm = pe.matmul(bank, ones_bf[:, 0:L], bias, start=False, stop=True)
                mm.then_inc(scored, 1)

            def turn_probs(geo, g, lot, u):
                unit = geo.group_units * g + geo.units * lot + u
                if u or lot:
                    pe.wait_ge(turn_kept, unit)
                pe.wait_ge(divided, unit + 1)
                for k in range(2):
                    n = 0
                    for j, _ in enumerate(geo.heads(u, k)):
                        for first, rows in geo.chunks:
                            col = (k * geo.bank_heads + j) * geo.keys + first
                            t = pe.transpose(ps_pt[0:rows, k, n * L:(n + 1) * L], probs[u % 2][:, col:col + rows],
                                             ident[0:L, 0:L])
                            n += 1
                t.then_inc(turned, 1)

            def mix_values(geo, g, lot, u):
                unit = geo.group_units * g + geo.units * lot + u
                pe.wait_ge(turn_kept, unit + 1)
                if u or lot:
                    pe.wait_ge(mix_kept, unit)
                i = geo.lots * g + lot
                pe.wait_ge(kept["v"], geo.v_tiles * i + (geo.v_tiles if geo.full else geo.batch(lot, u) + 1))
                n = 0
                for k in range(2):
                    for h in geo.heads(u, k):
                        r = HD * (h % 4)
                        out = ps_pv[r:r + HD, (0 if geo.full else k) * L:((0 if geo.full else k) + 1) * L]
                        for c, (first, rows) in enumerate(geo.chunks):
                            v = values[0:rows, c if geo.full else geo.batch(lot, u), h * HD:(h + 1) * HD]
                            mm = pe.matmul(out, v, probs_t[0:rows, n * L:(n + 1) * L], start=(c == 0),
                                           stop=(c == len(geo.chunks) - 1))
                            n += 1
                mm.then_inc(mixed_v, 1)

            def turn_back(g, b):
                if b:
                    pe.wait_ge(x1_ready, GB * g + b)
                pe.wait_ge(kept["o"], KD * g + KD)
                for k in range(KD):
                    t = pe.transpose(ps_tr[0:L, k * P:(k + 1) * P], gate_t[:, k, b * L:(b + 1) * L], ident[:, :])
                t.then_inc(back1_done, 1)

            def tail_part():
                mm_uses[:] = []
                for b in range(GB):
                    turn_x(0, b)
                for m in range(KD):
                    project_q(0, m)
                for m in range(KD):
                    project_k(tail, 0, m)

                def body(g, last):
                    mm_uses[:] = [("k", KD * g + KD - 1), ("k", KD * g + KD)]
                    for u in range(tail.units):
                        scores(tail, g, 0, u)
                        if u >= 2:
                            turn_probs(tail, g, 0, u - 2)
                        if u < GB:
                            project_v(tail, g, u)
                        else:
                            project_g(g, u - GB)
                        if u >= 2:
                            mix_values(tail, g, 0, u - 2)
                    n = g + 1
                    if not last:
                        for b in range(GB):
                            turn_x(n, b)
                            if b == 1:
                                turn_probs(tail, g, 0, 6)
                        mix_values(tail, g, 0, 6)
                        project_q(n, 0)
                        turn_probs(tail, g, 0, 7)
                        project_q(n, 1)
                        mix_values(tail, g, 0, 7)
                        project_q(n, 2)
                        project_q(n, 3)
                    else:
                        for u in (6, 7):
                            turn_probs(tail, g, 0, u)
                            mix_values(tail, g, 0, u)
                    pe.wait_ge(mix_kept, tail.units * g + tail.units)
                    for m in range(KD):
                        project_o(g, m)
                    for b in range(GB):
                        if not last and b < GB - 1:
                            project_k(tail, n, b)
                        turn_back(g, b)
                    if not last:
                        project_k(tail, n, GB - 1)
                    pe.wait_ge(x1_ready, GB * g + GB)

                pe.wait_ge(bias_made, 1)
                each_group(pe, body)

            def full_part():
                pe.wait_ge(bias_made, 1)
                with pe.Fori(0, NG) as g:
                    mm_uses[:] = []
                    for b in range(GB):
                        turn_x(g, b)
                    for m in range(KD):
                        project_q(g, m)
                    for m in range(KD):
                        project_g(g, m)
                    for lot in range(GB):
                        for m in range(KD):
                            project_k(full, GB * g + lot, m)
                        for c in range(full.v_tiles):
                            project_v(full, GB * g + lot, c)
                        for u in range(full.units):
                            scores(full, g, lot, u)
                            if u >= 2:
                                turn_probs(full, g, lot, u - 2)
                                mix_values(full, g, lot, u - 2)
                        for u in (6, 7):
                            turn_probs(full, g, lot, u)
                            mix_values(full, g, lot, u)
                    pe.wait_ge(mix_kept, full.group_units * g + full.group_units)
                    for m in range(KD):
                        project_o(g, m)
                    for b in range(GB):
                        turn_back(g, b)
                    pe.wait_ge(x1_ready, GB * g + GB)

            pe.wait_ge(const_loaded, 32)
            pe.wait_ge(filled, 5)
            branch(pe, tail_part, full_part)

            def turn_thought(i):
                wait_apart(pe, th_normed, i + 1)
                for k in range(KD):
                    t = pe.transpose(ps_pt[:, 1, k * B:(k + 1) * B], th_norm[:, k * P:(k + 1) * P], ident[0:B, 0:B])
                t.then_inc(tht_done, 1)

            turn_thought(0)
            pe.wait_ge(w_loaded["agg"], 16)
            pe.wait_ge(row_loaded, 16 * 7)
            pe.wait_ge(tht_ready, 1)
            for k in range(KD):
                pe.matmul(ps_pv[0:B, :], th_t[:, k, 0:B], agg[:, k, :], start=(k == 0), stop=False)
            pe.matmul(ps_pv[0:B, :], ones[:, :], agg_b[:, :], start=False, stop=True).then_inc(agg_done, 1)
            pe.wait_ge(w_loaded["d1"], 16)
            pe.wait_ge(w_loaded["d2"], 16)
            pe.wait_ge(w_loaded["fg"], 16)

            def turn_x2(s, b):
                if b:
                    pe.wait_ge(tr2_used, GB * s + b)
                pe.wait_ge(norm2_ready, GB * s + b + 1)
                for k in range(KD):
                    t = pe.transpose(ps_tr[:, k * L:(k + 1) * L], normed[:, b % 2, k * P:(k + 1) * P],
                                     ident[0:L, 0:L])
                t.then_inc(tr2_done, 1)

            def gate(s, m):
                if m >= 2:
                    pe.wait_ge(fg_kept, KD * s + m - 1)
                pe.wait_ge(tr2_used, GB * s + GB)
                for k in range(KD):
                    mm = pe.matmul(ps_mm[m % 2][:, 0:GL], fg[:, k, m * P:(m + 1) * P], x2_t[:, k, :],
                                   start=(k == 0), stop=(k == KD - 1))
                mm.then_inc(fg_done, 1)

            with pe.Fori(0, STEPS) as s:
                turn_x2(s, 0)
                turn_x2(s, 1)
                turn_thought(s + 1)
                turn_x2(s, 2)
                pe.wait_ge(tht_ready, s + 2)
                for k in range(KD):
                    for j in range(FJ):
                        mm = pe.matmul(ps_s[32 * j:32 * j + 32, 0, :], th_t[:, k, :], d1[:, k, j * D:(j + 1) * D],
                                       start=(k == 0), stop=(k == KD - 1))
                mm.then_inc(up_done, 1)
                turn_x2(s, 3)
                pe.wait_ge(up_kept, s + 1)
                for i in range(KD):
                    t = pe.transpose(ps_pt[:, 0, i * P:(i + 1) * P], hid[:, i * P:(i + 1) * P], ident[:, :])
                t.then_inc(upt_done, 1)
                gate(s, 0)
                pe.wait_ge(hid_ready, s + 1)
                for i in range(KD):
                    for j in range(FJ):
                        mm = pe.matmul(ps_s[32 * j:32 * j + 32, 1, :], hid_t[:, KD * i + j, :], d2[:, KD * j + i, :],
                                       start=(i == 0), stop=(i == KD - 1))
                mm.then_inc(down_done, 1)
                gate(s, 1)
                pe.matmul(ps_pv[0:B, :], ones[:, :], d2_b[:, :], start=True, stop=False)
                pe.wait_ge(down_kept, s + 1)
                pe.matmul(ps_pv[0:B, :], pick[:, :], parts, start=False, stop=True).then_inc(sum_done, 1)
                gate(s, 2)
                gate(s, 3)
            pe.wait_ge(th_ready, STEPS + 1)
            for k in range(KD):
                t = pe.transpose(ps_pt[:, 1, k * B:(k + 1) * B], thought[:, k * P:(k + 1) * P], ident[0:B, 0:B])
            t.then_inc(tht_done, 1)
            pe.wait_ge(w_loaded["bc"], 16)
            pe.wait_ge(tht_ready, STEPS + 2)
            for m in range(KD):
                for k in range(KD):
                    mm = pe.matmul(ps_pv[:, m * B:(m + 1) * B], bc[:, k, m * P:(m + 1) * P], th_t[:, k, 0:B],
                                   start=(k == 0), stop=(k == KD - 1))
            mm.then_inc(bc_done, 1)

            def back(g, s):
                i = GB * g + s
                pe.wait_ge(lifted, i + 1)
                if s >= 2 or not isinstance(g, int) or g:
                    pe.wait_ge(o_ready, i - 1)
                for k in range(KD):
                    t = pe.transpose(ps_mm[s % 2][0:L, k * P:(k + 1) * P], lift[:, s % 2, k, :], ident[:, :])
                t.then_inc(back_done, 1)

            each_out(pe, back)

        @block.scalar
        def _(act):
            def keep_q(n, m):
                act.wait_ge(done["q"], KD * n + m + 1)
                act.activation(q_t[:, m, :], ps_mm[m % 2][:, 0:GL], ACT.Copy).then_inc(kept["q"], 1)

            def keep_g(n, m):
                act.wait_ge(done["g"], KD * n + m + 1)
                act.activation(gate_t[:, m, :], ps_mm[m % 2][:, 0:GL], ACT.Tanh, scale=0.5).then_inc(kept["g"], 1)

            def keep_k(geo, i, m, bank):
                act.wait_ge(done["k"], KD * i + m + 1)
                for j in range(4):
                    r = slice(HD * j, HD * j + HD)
                    if geo.full:
                        dst = keys[r, (4 * m + j) * M:(4 * m + j + 1) * M]
                        src = bank[r, 0:M]
                    else:
                        dst = keys[r, 0:GB * NH * TAIL].rearrange("p (b h n) -> p b h n", b=GB, h=NH)[:, :, 4 * m + j, :]
                        src = bank[r, 0:GB * TAIL].rearrange("p (b n) -> p b n", b=GB)
                    c = act.activation(dst, src, ACT.Copy)
                c.then_inc(kept["k"], 1)

            def raise_(geo, g, lot, u):
                unit = geo.group_units * g + geo.units * lot + u
                act.wait_ge(shifted, unit + 1)
                w = geo.unit_heads * geo.keys
                act.activation(probs[u % 2][:, 0:w], probs[u % 2][:, 0:w], ACT.Exp, scale=SCALE).then_inc(raised, 1)

            def keep_turned(geo, g, lot, u):
                unit = geo.group_units * g + geo.units * lot + u
                act.wait_ge(turned, unit + 1)
                if geo.full:
                    whole = [c for c in geo.chunks if c[1] == P]
                    w, rest = len(whole) * L, geo.chunks[-1][1]
                    dst = probs_t[:, 0:6 * L].rearrange("p (k n) -> p k n", k=2)
                    act.activation(dst[:, :, 0:w], ps_pt[:, :, 0:w], ACT.Copy)
                    act.activation(dst[0:rest, :, w:w + L], ps_pt[0:rest, :, w:w + L], ACT.Copy).then_inc(turn_kept, 1)
                else:
                    dst = probs_t[0:TAIL, :].rearrange("p (k n) -> p k n", k=2)
                    act.activation(dst, ps_pt[0:TAIL, :, 0:4 * L], ACT.Copy).then_inc(turn_kept, 1)

            def keep_mixed(geo, g, lot, u):
                unit = geo.group_units * g + geo.units * lot + u
                b = geo.batch(lot, u)
                act.wait_ge(mixed_v, unit + 1)
                if geo.full:
                    r = slice(64 * (u % 2), 64 * (u % 2) + 64)
                    dst, src = att_t[r, u // 2, b * L:(b + 1) * L], ps_pv[r, 0:L]
                else:
                    t = 2 * (u % 2)
                    dst = att_t[:, t:t + 2, b * L:(b + 1) * L]
                    src = ps_pv[:, 0:2 * L].rearrange("p (k n) -> p k n", k=2)
                act.activation(dst, src, ACT.Copy).then_inc(mix_kept, 1)

            def tail_part():
                act.wait_ge(zeroed, 1)
                for m in range(KD):
                    keep_q(0, m)
                for m in range(KD):
                    keep_k(tail, 0, m, ps_mm[m % 2])

                def body(g, last):
                    for u in range(tail.units):
                        if u >= 2:
                            keep_turned(tail, g, 0, u - 2)
                        raise_(tail, g, 0, u)
                        if u >= GB:
                            keep_g(g, u - GB)
                        if u >= 2:
                            keep_mixed(tail, g, 0, u - 2)
                    keep_turned(tail, g, 0, 6)
                    keep_mixed(tail, g, 0, 6)
                    if last:
                        keep_turned(tail, g, 0, 7)
                        keep_mixed(tail, g, 0, 7)
                        return
                    n = g + 1
                    keep_q(n, 0)
                    keep_turned(tail, g, 0, 7)
                    keep_q(n, 1)
                    keep_mixed(tail, g, 0, 7)
                    keep_q(n, 2)
                    keep_q(n, 3)
                    for m in range(KD):
                        keep_k(tail, n, m, ps_mm[m % 2])

                each_group(act, body)

            def full_part():
                act.wait_ge(zeroed, 1)
                with act.Fori(0, NG) as g:
                    for m in range(KD):
                        keep_q(g, m)
                    for m in range(KD):
                        keep_g(g, m)
                    uses = 2 * KD
                    for lot in range(GB):
                        for m in range(KD):
                            keep_k(full, GB * g + lot, m, ps_mm[(uses + m) % 2])
                        uses += KD + full.v_tiles
                        for u in range(full.units):
                            raise_(full, g, lot, u)
                            if u >= 2:
                                keep_turned(full, g, lot, u - 2)
                                keep_mixed(full, g, lot, u - 2)
                        for u in (6, 7):
                            keep_turned(full, g, lot, u)
                            keep_mixed(full, g, lot, u)

            branch(act, tail_part, full_part)

            def keep_x2(s, b):
                act.wait_ge(tr2_done, GB * s + b + 1)
                act.activation(x2_t[:, :, b * L:(b + 1) * L],
                               ps_tr[:, 0:GL].rearrange("p (k n) -> p k n", k=KD), ACT.Copy).then_inc(tr2_used, 1)

            def keep_gate(s, m):
                act.wait_ge(fg_done, KD * s + m + 1)
                act.activation(gates[:, m, bass.ds(s * GL, GL)], ps_mm[m % 2][:, 0:GL], ACT.Tanh,
                               bias=half_gate_b[:, m:m + 1], scale=0.5).then_inc(fg_kept, 1)

            act.wait_ge(half_made, 1)
            with act.Fori(0, STEPS) as s:
                keep_x2(s, 0)
                keep_x2(s, 1)
                keep_x2(s, 2)
                act.wait_ge(up_done, s + 1)
                act.activation(hid, ps_s[:, 0, :], ACT.Copy).then_inc(up_kept, 1)
                keep_x2(s, 3)
                act.wait_ge(z_ready, s + 1)
                act.activation(hid_t[:, :, 0:B], z_t.rearrange("p (f b) -> p f b", f=FS),
                               ACT.Gelu).then_inc(hid_ready, 1)
                keep_gate(s, 0)
                act.wait_ge(down_done, s + 1)
                act.activation(parts, ps_s[:, 1, :], ACT.Copy).then_inc(down_kept, 1)
                keep_gate(s, 1)
                keep_gate(s, 2)
                keep_gate(s, 3)

            def norm_out(g, s):
                act.wait_ge(o_shift_ready, GB * g + s + 1)
                act.activation(mixed[:, s, :], mixed[:, s, :], ACT.Identity, bias=o_shift[:, s:s + 1],
                               scale=o_rstd[:, s:s + 1]).then_inc(o_normed, 1)

            each_out(act, norm_out)

        @block.vector
        def _(dve):
            dve.memset(flag_a[:, :], 0.0).then_inc(flag_step, 1)
            dve.wait_ge(flag_step, 1)
            dve.wait_ge(mask_loaded, 16)
            dve.tensor_reduce(flag_a[0:B, 0:1], mask_any[:, :], AX_X, ALU.max).then_inc(flag_step, 1)
            dve.wait_ge(flag_step, 2)
            dve.transpose(flag_b[:, :], flag_a[:, :]).then_inc(flag_step, 1)
            dve.wait_ge(flag_step, 3)
            dve.tensor_reduce(flag[0:1, 0:1], flag_b[0:1, :], AX_X, ALU.max).then_inc(flag_set, 1)

            def statistics(g, b):
                if isinstance(g, int) and g == 0:
                    dve.wait_ge(x_first_loaded, 16)
                else:
                    dve.wait_ge(x_rest_loaded, 16)
                dve.bn_stats(st[:, b, :], x[:, bass.ds(GB * g + b, 1), :].rearrange("p a n -> p (a n)")
                             ).then_inc(st_made, 1)
                wait_apart(dve, st_made, GB * g + b + 1)
                dve.bn_aggr(mv[:, b, :], st[:, b, :]).then_inc(mv_made, 1)

            def variance(g):
                dve.wait_ge(mv_made, GB * g + GB)
                dve.tensor_scalar(vr[:, :].unsqueeze(2), mv[:, :, 1:2],
                                  1.0 + EPS_IN, EPS_LN * EPS_IN, ALU.mult, ALU.add).then_inc(var_ready, 1)

            def normalise(g, b):
                if b >= 2:
                    dve.wait_ge(xt_done, GB * g + b - 1)
                if b == 0:
                    dve.wait_ge(rstd_ready, g + 1)
                i = GB * g + b
                dve.tensor_scalar(normed[:, b % 2, :], x[:, bass.ds(i, 1), :].rearrange("p a n -> p (a n)"),
                                  mv[:, b, 0:1], rstd[:, b:b + 1],
                                  ALU.subtract, ALU.mult).then_inc(norm_ready, 1)

            def keep_x(g, b):
                dve.wait_ge(xt_done, GB * g + b + 1)
                dve.tensor_tensor(x_t[:, :, b * L:(b + 1) * L], ps_tr[:, 0:GL].rearrange("p (k n) -> p k n", k=KD),
                                  norm_w.unsqueeze(2).to_broadcast([P, KD, L]), ALU.mult).then_inc(xt_kept, 1)

            def turn_group(g):
                for b in range(GB):
                    normalise(g, b)
                    if b >= 1:
                        keep_x(g, b - 1)
                keep_x(g, GB - 1)

            def make_bias(geo):
                n = B * geo.keys
                dve.wait_ge(mask_row_loaded, 16)
                dve.tensor_scalar(mask_bias[:, 0:n], mask_row[:, 0:n], -MASKED, MASKED, ALU.mult,
                                  ALU.add).then_inc(bias_made, 1)

            def scores_view(geo):
                return ps_s[0:L, :, 0:geo.bank_heads * geo.keys].rearrange("p k (h n) -> p k h n", h=geo.bank_heads)

            def probs_view(geo, u):
                return probs[u % 2][:, 0:geo.unit_heads * geo.keys].rearrange(
                    "p (k h n) -> p k h n", k=2, h=geo.bank_heads)

            def per_head(t, geo, u):
                return t[:, u % 2, 0:geo.unit_heads]

            def subtract_max(geo, g, lot, u):
                unit = geo.group_units * g + geo.units * lot + u
                dve.wait_ge(scored, unit + 1)
                if u >= 2 or lot:
                    dve.wait_ge(weighted, unit - 1)
                mx = per_head(row_max, geo, u)
                mx4 = mx.rearrange("p (k h) -> p k h", k=2)
                dve.tensor_reduce(mx4, scores_view(geo), AX_X, ALU.max).then_inc(maxed, 1)
                dve.wait_ge(maxed, unit + 1)
                if u >= 2 or lot:
                    dve.wait_ge(turned, unit - 1)
                dve.tensor_tensor(probs_view(geo, u), scores_view(geo),
                                  mx4.unsqueeze(3).to_broadcast([L, 2, geo.bank_heads, geo.keys]),
                                  ALU.subtract).then_inc(shifted, 1)

            def invert_sum(geo, g, lot, u):
                unit = geo.group_units * g + geo.units * lot + u
                dve.wait_ge(raised, unit + 1)
                sm, inv, mx = (per_head(t, geo, u) for t in (row_sum, row_inv, row_max))
                dve.tensor_reduce(sm.rearrange("p (k h) -> p k h", k=2), probs_view(geo, u), AX_X,
                                  ALU.add).then_inc(summed, 1)
                dve.wait_ge(summed, unit + 1)
                dve.reciprocal(inv, sm).then_inc(inverted, 1)
                dve.wait_ge(inverted, unit + 1)
                dve.scalar_tensor_tensor(out=inv, in0=mx, scalar=ALIVE, in1=inv, op0=ALU.is_gt,
                                         op1=ALU.mult).then_inc(weighted, 1)

            def keep_v(geo, i, c, bank):
                rows = geo.chunks[c][1] if geo.full else TAIL
                dve.wait_ge(done["v"], geo.v_tiles * i + c + 1)
                dve.tensor_copy(values[0:rows, c, :], bank[0:rows, :]).then_inc(kept["v"], 1)

            def gate_output(g, m):
                dve.wait_ge(done["o"], KD * g + m + 1)
                if m == 0:
                    dve.wait_ge(kept["g"], KD * g + KD)
                dve.scalar_tensor_tensor(out=gate_t[:, m, :], in0=gate_t[:, m, :], scalar=1.0,
                                         in1=ps_mm[m % 2][:, 0:GL], op0=ALU.add, op1=ALU.mult).then_inc(kept["o"], 1)

            def add_attention(g, b):
                i = GB * g + b
                dve.wait_ge(back1_done, i + 1)
                row = x[:, bass.ds(i, 1), :].rearrange("p a n -> p (a n)")
                dve.scalar_tensor_tensor(out=row, in0=ps_tr[0:L, :], scalar=0.5, in1=row, op0=ALU.mult,
                                         op1=ALU.add).then_inc(x1_ready, 1)
                wait_apart(dve, x1_ready, i + 1)
                dve.bn_stats(st1[:, b, :], row).then_inc(st1_made, 1)
                wait_apart(dve, st1_made, i + 1)
                dve.bn_aggr(mv1[:, b, :], st1[:, b, :]).then_inc(mv1_made, 1)
                if b == GB - 1:
                    dve.wait_ge(mv1_made, i + 1)
                    dve.tensor_copy(mean1[:, bass.ds(GB * g, GB)].unsqueeze(2), mv1[:, :, 0:1]
                                    ).then_inc(mean1_ready, 1)
                    dve.tensor_scalar(vr1[:, bass.ds(GB * g, GB)].unsqueeze(2), mv1[:, :, 1:2],
                                      EPS_LN, None, ALU.add).then_inc(var1_ready, 1)

            for b in range(GB):
                statistics(0, b)
            variance(0)
            dve.wait_ge(const_loaded, 32)

            def tail_part():
                make_bias(tail)
                turn_group(0)

                def body(g, last):
                    n = g + 1
                    for u in range(tail.units):
                        subtract_max(tail, g, 0, u)
                        if u >= 1:
                            invert_sum(tail, g, 0, u - 1)
                        if u < GB:
                            keep_v(tail, g, u, ps_mm[u % 2])
                        elif not last:
                            statistics(n, u - GB)
                    if not last:
                        variance(n)
                    invert_sum(tail, g, 0, 7)
                    if not last:
                        turn_group(n)
                    for m in range(KD):
                        gate_output(g, m)
                    for b in range(GB):
                        add_attention(g, b)

                each_group(dve, body)

            def full_part():
                make_bias(full)

                def body(g, last):
                    turn_group(g)
                    uses = 2 * KD
                    for lot in range(GB):
                        uses += KD
                        for c in range(full.v_tiles):
                            keep_v(full, GB * g + lot, c, ps_mm[(uses + c) % 2])
                        uses += full.v_tiles
                        for u in range(full.units):
                            subtract_max(full, g, lot, u)
                            if u >= 1:
                                invert_sum(full, g, lot, u - 1)
                        invert_sum(full, g, lot, 7)
                    for m in range(KD):
                        gate_output(g, m)
                    for b in range(GB):
                        add_attention(g, b)
                    if not last:
                        for b in range(GB):
                            statistics(g + 1, b)
                        variance(g + 1)

                each_group(dve, body)

            branch(dve, tail_part, full_part)

            def measure(src, i, scale, eps):
                dve.bn_stats(th_st[:, :], src).then_inc(th_st_made, 1)
                wait_apart(dve, th_st_made, i + 1)
                dve.bn_aggr(th_mv[:, :], th_st[:, :]).then_inc(th_mv_made, 1)
                dve.wait_ge(th_mv_made, i + 1)
                dve.tensor_scalar(th_var[:, :], th_mv[:, 1:2], scale, eps, ALU.mult, ALU.add).then_inc(th_var_ready, 1)

            def normalise_thought(src, i):
                dve.wait_ge(th_rstd_ready, i + 1)
                dve.tensor_scalar(th_norm[:, :], src, th_mv[:, 0:1], th_rstd[:, 0:1], ALU.subtract,
                                  ALU.mult).then_inc(th_normed, 1)

            def scale_thought(i, gamma, beta):
                dve.wait_ge(tht_done, i + 1)
                dve.tensor_tensor(th_t0[:, :, :], ps_pt[:, 1, 0:KD * B].rearrange("p (k n) -> p k n", k=KD),
                                  gamma.unsqueeze(2).to_broadcast([P, KD, B]), ALU.mult).then_inc(tht_scaled, 1)
                dve.wait_ge(tht_scaled, i + 1)
                dve.tensor_tensor(th_t[:, :, 0:B], th_t0[:, :, :], beta.unsqueeze(2).to_broadcast([P, KD, B]),
                                  ALU.add).then_inc(tht_ready, 1)

            def normalise2(s, b):
                if b >= 2:
                    dve.wait_ge(tr2_done, GB * s + b - 1)
                if b == 0:
                    dve.wait_ge(rstd1_ready, s + 1)
                i = GB * s + b
                dve.tensor_scalar(normed[:, b % 2, :], x[:, bass.ds(i, 1), :].rearrange("p a n -> p (a n)"),
                                  mean1[:, bass.ds(i, 1)], rstd1[:, bass.ds(i, 1)],
                                  ALU.subtract, ALU.mult).then_inc(norm2_ready, 1)

            dve.wait_ge(last_row_loaded, 16)
            measure(last_row[:, :], 0, 1.0 + EPS_IN, EPS_LN * EPS_IN)
            normalise_thought(last_row[:, :], 0)
            dve.wait_ge(filled, 5)
            scale_thought(0, in_gamma, in_beta)
            dve.wait_ge(agg_done, 1)
            dve.tensor_copy(thought[:, :], ps_pv[0:B, :]).then_inc(th_ready, 1)
            dve.wait_ge(row_loaded, 16 * 7)
            with dve.Fori(0, STEPS) as s:
                wait_apart(dve, th_ready, s + 1)
                measure(thought[:, :], s + 1, 1.0, EPS_IN)
                normalise2(s, 0)
                normalise2(s, 1)
                normalise_thought(thought[:, :], s + 1)
                normalise2(s, 2)
                scale_thought(s + 1, pn_gamma, pn_beta)
                normalise2(s, 3)
                dve.wait_ge(upt_done, s + 1)
                dve.tensor_tensor(z_t.rearrange("p (i j b) -> p i j b", i=KD, j=FJ),
                                  ps_pt[:, 0, :].rearrange("p (i j b) -> p i j b", i=KD, j=FJ)[:, :, :, 0:B],
                                  d1b[:, :, :].unsqueeze(3).to_broadcast([P, KD, FJ, B]), ALU.add).then_inc(z_ready, 1)
                dve.wait_ge(sum_done, s + 1)
                dve.tensor_tensor(thought[:, :], ps_pv[0:B, :], thought[:, :], ALU.add).then_inc(th_ready, 1)
            dve.wait_ge(tht_done, STEPS + 2)
            dve.tensor_copy(th_t[:, :, 0:B], ps_pt[:, 1, 0:KD * B].rearrange("p (k n) -> p k n", k=KD)
                            ).then_inc(tht_ready, 1)
            dve.wait_ge(bc_done, 1)
            for m in range(KD):
                dve.tensor_scalar(bc_half[:, m, :], ps_pv[:, m * B:(m + 1) * B], bc_b[:, m:m + 1], 0.5, ALU.add,
                                  ALU.mult).then_inc(bc_ready, 1)
            dve.wait_ge(bc_ready, KD)
            dve.wait_ge(fg_kept, KD * NG)

            def raise_gate(g, s):
                i = GB * g + s
                dve.scalar_tensor_tensor(out=lift[:, s % 2, :, :], in0=gates[:, :, bass.ds(i * L, L)], scalar=1.0,
                                         in1=bc_half[:, :, bass.ds(i, 1)].to_broadcast([P, KD, L]), op0=ALU.add,
                                         op1=ALU.mult).then_inc(lifted, 1)

            def add_x(g, s):
                i = GB * g + s
                dve.wait_ge(o_biased, i + 1)
                dve.tensor_tensor(final[:, s, :], final[:, s, :], x[:, bass.ds(i, 1), :].rearrange("p a n -> p (a n)"),
                                  ALU.add).then_inc(out_ready, 1)

            def output(g, s):
                i = GB * g + s
                if not (isinstance(g, int) and g == NG - 1 and s == GB - 1):
                    raise_gate(g + (s + 1) // GB, (s + 1) % GB)
                dve.wait_ge(back_done, i + 1)
                dve.scalar_tensor_tensor(out=mixed[:, s, :], in0=x[:, bass.ds(i, 1), :].rearrange("p a n -> p (a n)"),
                                         scalar=rstd1[:, bass.ds(i, 1)], in1=ps_mm[s % 2][0:L, :], op0=ALU.mult,
                                         op1=ALU.add).then_inc(o_ready, 1)
                wait_apart(dve, o_ready, i + 1)
                dve.bn_stats(o_st[:, s, :], mixed[:, s, :]).then_inc(o_st_made, 1)
                wait_apart(dve, o_st_made, i + 1)
                dve.bn_aggr(o_mv[:, s, :], o_st[:, s, :]).then_inc(o_mv_made, 1)
                dve.wait_ge(o_mv_made, i + 1)
                dve.tensor_scalar(o_var[:, s:s + 1], o_mv[:, s, 1:2], EPS_IN, None, ALU.add).then_inc(o_var_ready, 1)
                if not (isinstance(g, int) and g == 0 and s < 2):
                    add_x(g if s >= 2 else g - 1, (s - 2) % GB)
                dve.wait_ge(o_rstd_ready, i + 1)
                dve.scalar_tensor_tensor(out=o_shift[:, s:s + 1], in0=o_mv[:, s, 0:1], scalar=-1.0,
                                         in1=o_rstd[:, s:s + 1], op0=ALU.mult, op1=ALU.mult).then_inc(o_shift_ready, 1)

            raise_gate(0, 0)
            each_out(dve, output)
            add_x(NG - 1, GB - 2)
            add_x(NG - 1, GB - 1)

        @block.gpsimd
        def _(pool):
            for dst, v in ((ones_bf, 1.0), (ones, 1.0), (minus_half, -0.5), (th_t, 0.0), (hid_t, 0.0)):
                pool.memset(dst[:], v).then_inc(filled, 1)
            pool.wait_ge(filled, 5)

            def rstd_of(g):
                pool.wait_ge(var_ready, g + 1)
                pool.tensor_tensor(rstd[:, :], vr[:, :], minus_half[:, 0:GB], ALU.pow).then_inc(rstd_ready, 1)

            def rstd1_of(g):
                pool.wait_ge(var1_ready, g + 1)
                pool.tensor_tensor(rstd1[:, bass.ds(GB * g, GB)], vr1[:, bass.ds(GB * g, GB)], minus_half[:, 0:GB],
                                   ALU.pow).then_inc(rstd1_ready, 1)

            def divide(geo, g, lot, u):
                unit = geo.group_units * g + geo.units * lot + u
                pool.wait_ge(weighted, unit + 1)
                w = probs[u % 2][:, 0:geo.unit_heads * geo.keys].rearrange("p (h n) -> p h n", h=geo.unit_heads)
                inv = row_inv[:, u % 2, 0:geo.unit_heads].unsqueeze(2).to_broadcast([L, geo.unit_heads, geo.keys])
                pool.tensor_tensor(w, w, inv, ALU.mult).then_inc(divided, 1)

            pool.memset(keys, 0.0).then_inc(zeroed, 1)
            rstd_of(0)
            pool.wait_ge(const_loaded, 32)
            pool.tensor_scalar(half_gate_b[:, :], gate_b, 0.5, None, ALU.mult).then_inc(half_made, 1)

            def tail_part():
                def body(g, last):
                    for u in range(tail.units - 1):
                        divide(tail, g, 0, u)
                    if not last:
                        rstd_of(g + 1)
                    divide(tail, g, 0, tail.units - 1)
                    rstd1_of(g)

                each_group(pool, body)

            def full_part():
                def body(g, last):
                    for lot in range(GB):
                        for u in range(full.units):
                            divide(full, g, lot, u)
                    rstd1_of(g)
                    if not last:
                        rstd_of(g + 1)

                each_group(pool, body)

            branch(pool, tail_part, full_part)

            def thought_rstd(i):
                pool.wait_ge(th_var_ready, i + 1)
                pool.tensor_tensor(th_rstd[:, :], th_var[:, :], minus_half[0:B, 0:1], ALU.pow).then_inc(th_rstd_ready, 1)

            thought_rstd(0)
            with pool.Fori(0, STEPS) as s:
                thought_rstd(s + 1)
            pool.wait_ge(row_loaded, 16 * 7)

            def affine(g, s):
                i = GB * g + s
                pool.wait_ge(o_normed, i + 1)
                if not (isinstance(g, int) and g == 0):
                    pool.wait_ge(stored[s], 16 * g)
                pool.tensor_tensor(final[:, s, :], mixed[:, s, :], gamma_row[:, :], ALU.mult).then_inc(o_scaled, 1)
                pool.wait_ge(o_scaled, i + 1)
                pool.tensor_tensor(final[:, s, :], final[:, s, :], beta_row[:, :], ALU.add).then_inc(o_biased, 1)

            def out_stage(g, s):
                i = GB * g + s
                pool.wait_ge(o_var_ready, i + 1)
                pool.tensor_tensor(o_rstd[:, s:s + 1], o_var[:, s:s + 1], minus_half[:, 0:1],
                                   ALU.pow).then_inc(o_rstd_ready, 1)
                if not (isinstance(g, int) and g == 0 and s == 0):
                    affine(g if s else g - 1, (s - 1) % GB)

            each_out(pool, out_stage)
            affine(NG - 1, GB - 1)


def kernel(**inputs):
    import numpy as np
    import concourse.bacc as bacc
    from concourse.bass_utils import run_bass_kernel_spmd

    def arr(name):
        return np.asarray(inputs[name])

    def sliced(w):
        return w.reshape(-1, P, w.shape[-1]).transpose(1, 0, 2)

    def per_partition(v):
        return v.reshape(-1, P).T

    ffn = "L0_ffn_"
    ctx, mask = arr("ctx_2048"), arr("mask_BxS2_bk0")
    ctx_t = ctx.transpose(2, 0, 1).reshape(KD, P, B, M)
    last = ctx_t[:, :, :, HEAD_ROWS:].reshape(KD, P, NG, GB, TAIL)
    arrays = {
        "x": arr("x"),
        "ctx_tail": last.transpose(2, 1, 0, 3, 4).reshape(NG, P, KD * GB * TAIL),
        "ctx_full": ctx_t.transpose(2, 1, 0, 3).reshape(B, P, KD * M),
        "mask": mask,
        "mask_row_tail": mask[:, HEAD_ROWS:].reshape(1, B * TAIL),
        "mask_row_full": mask.reshape(1, B * M),
        "wq": sliced(arr("L0_xattn_wq").T), "wk": sliced(arr("L0_xattn_wk").T),
        "wv": sliced(arr("L0_xattn_wv").T), "wo": sliced(arr("L0_xattn_wo").T),
        "wg": sliced(arr("L0_xattn_wg").T), "fg": sliced(arr(ffn + "gate_w")),
        "agg": sliced(arr(ffn + "agg_w")), "bc": sliced(arr(ffn + "bc_w")),
        "d1": sliced(arr(ffn + "d1_w")), "d2": sliced(arr(ffn + "d2_w")),
        "vecs": np.stack([per_partition(arr(n)) for n in (
            "L0_xattn_norm_w", ffn + "in_gamma", ffn + "in_beta", ffn + "gate_b", ffn + "bc_b")], axis=1),
        "pn_vecs": np.stack([per_partition(arr(ffn + n)) for n in ("pn_gamma", "pn_beta")], axis=1),
        "d1b": arr(ffn + "d1_b").reshape(FJ, KD, P).transpose(2, 1, 0),
        "agg_b": arr(ffn + "agg_b")[None], "d2_b": arr(ffn + "d2_b")[None],
        "out_gamma": arr(ffn + "out_gamma")[None], "out_beta": arr(ffn + "out_beta")[None],
        "ident": np.eye(P, dtype=np.float32),
        "pick": np.array([[float(r % 32 == b) for b in range(B)] for r in range(P)], np.float32),
    }
    nc = bacc.Bacc("TRN2", target_bir_lowering=False, num_devices=1)
    feeds, a = {}, {}
    for name, v in arrays.items():
        v = np.ascontiguousarray(v)
        feeds[f"in_{name}"] = v
        a[name] = nc.dram_tensor(f"in_{name}", v.shape, mybir.dt.from_np(v.dtype), kind="ExternalInput").ap()
    a["out"] = nc.dram_tensor("out_0", (B, L, D), F32, kind="ExternalOutput").ap()
    xattn_ffn(nc, a)
    r = run_bass_kernel_spmd(nc, [feeds], core_ids=[0])
    return r.results[0]["out_0"]
```

```python
from contextlib import ExitStack

import concourse.bass as bass
from concourse import mybir

F32 = mybir.dt.float32
BF16 = mybir.dt.bfloat16
I32 = mybir.dt.int32
ALU = mybir.AluOpType
ACT = mybir.ActivationFunctionType
AX_X = mybir.AxisListType.X

B, L, D, M = 16, 100, 512, 361
NH, HD = 16, 32
P = 128
KD = D // P
GB = 4
NG = B // GB
GL = GB * L
F = 2048
FJ = F // D
FS = F // P
STEPS = 4
TAIL = M // 4
HEAD_ROWS = M - TAIL
SCALE = float(HD) ** -0.5
EPS_LN, EPS_IN = 1e-5, 1e-6
MASKED = -1e30
ALIVE = -5e29


class Geometry:

    def __init__(self, full):
        self.full = full
        self.keys = M if full else TAIL
        self.bank_heads = 1 if full else KD
        self.unit_heads = 2 * self.bank_heads
        self.units = 8
        self.lots = GB if full else 1
        self.group_units = self.units * self.lots
        self.lot_keys = self.keys * (1 if full else GB)
        self.chunks = [(c, min(P, self.keys - c)) for c in range(0, self.keys, P)]
        self.v_tiles = len(self.chunks) if full else GB

    def batch(self, lot, u):
        return lot if self.full else u // 2

    def heads(self, u, k):
        if self.full:
            return [2 * u + k]
        first = 8 * (u % 2) + 4 * k
        return list(range(first, first + 4))


def xattn_ffn(nc, a):
    ctx = ExitStack()
    with ctx:
        def sb(name, shape, dt=F32):
            return ctx.enter_context(nc.sbuf_tensor(name, shape, dt))

        def sem(name):
            return ctx.enter_context(nc.semaphore(name))

        x = sb("x", [L, B, D])
        w_arena = sb("w_arena", [P, 4 * KD * D])
        kv_arena = sb("kv_arena", [P, FS * D])
        t_arena = sb("t_arena", [P, KD * B * L])
        c_arena = sb("c_arena", [P, 3200])
        wo = sb("wo", [P, KD, D])
        fg = sb("fg", [P, KD, D])
        agg = sb("agg", [P, KD, D])
        bc = sb("bc", [P, KD, D])
        probs_t = sb("probs_t", [P, 800])
        normed = sb("normed", [L, 2, D])
        gamma_row = sb("gamma_row", [L, D])
        beta_row = sb("beta_row", [L, D])
        mask_bias = sb("mask_bias", [1, B * M], BF16)
        mask_any = sb("mask_any", [B, HEAD_ROWS], mybir.dt.uint8)
        flag_a = sb("flag_a", [32, 32])
        flag_b = sb("flag_b", [32, 32])
        flag = sb("flag", [1, 4], I32)
        ident = sb("ident", [P, P])
        pick = sb("pick", [P, B])
        ones_bf = sb("ones_bf", [1, P], BF16)
        ones = sb("ones", [1, B])
        minus_half = sb("minus_half", [L, B])
        vecs = sb("vecs", [P, 5, KD])
        pn_vecs = sb("pn_vecs", [P, 2, KD])
        d1b = sb("d1b", [P, KD, FJ])
        agg_b = sb("agg_b", [1, D])
        d2_b = sb("d2_b", [1, D])
        half_gate_b = sb("half_gate_b", [P, KD])
        st = sb("st", [L, GB, 6])
        mv = sb("mv", [L, GB, 2])
        vr = sb("vr", [L, GB])
        rstd = sb("rstd", [L, GB])
        st1 = sb("st1", [L, GB, 6])
        mv1 = sb("mv1", [L, GB, 2])
        mean1 = sb("mean1", [L, B])
        vr1 = sb("vr1", [L, B])
        rstd1 = sb("rstd1", [L, B])
        row_max = sb("row_max", [L, 2, 8])
        row_sum = sb("row_sum", [L, 2, 8])
        row_inv = sb("row_inv", [L, 2, 8])
        last_row = sb("last_row", [B, D])
        thought = sb("thought", [B, D])
        th_norm = sb("th_norm", [B, D])
        th_st = sb("th_st", [B, 6])
        th_mv = sb("th_mv", [B, 2])
        th_var = sb("th_var", [B, 1])
        th_rstd = sb("th_rstd", [B, 1])
        th_t0 = sb("th_t0", [P, KD, B])
        th_t = sb("th_t", [P, KD, 32])
        hid_t = sb("hid_t", [P, FS, 32])
        bc_half = sb("bc_half", [P, KD, B])
        o_sum, o_minus, o_mean, o_var, o_var_eps, o_rstd = (
            sb(n, [L, GB]) for n in ("o_sum", "o_minus", "o_mean", "o_var", "o_var_eps", "o_rstd"))

        wk, wv, wq, wg = (w_arena[:, i * KD * D:(i + 1) * KD * D].rearrange("p (k n) -> p k n", k=KD)
                          for i in range(4))
        d1 = w_arena[:, :].rearrange("p (k n) -> p k n", k=KD)
        KCOLS = NH * M
        keys = kv_arena[:, 0:KCOLS]
        values = kv_arena[:, KCOLS:KCOLS + GB * D].rearrange("p (c n) -> p c n", c=GB)
        d2 = kv_arena[:, :].rearrange("p (k n) -> p k n", k=FS)
        x_t, q_t, gate_t, att_t = (t_arena[:, i * KD * GL:(i + 1) * KD * GL].rearrange("p (k n) -> p k n", k=KD)
                                   for i in range(4))
        mask_row = att_t[0:1, :, :].rearrange("p k n -> p (k n)").bitcast(mybir.dt.uint8)
        gates = t_arena[:, :].rearrange("p (k n) -> p k n", k=KD)
        ctx_t = c_arena[:, 0:KD * M]
        UNIT = 722
        probs = [c_arena[0:L, KD * M + i * UNIT:KD * M + (i + 1) * UNIT] for i in range(2)]
        x2_t = c_arena[:, 0:KD * GL].rearrange("p (k n) -> p k n", k=KD)
        hid = parts = c_arena[:, 1600:1600 + D]
        z_t = c_arena[:, 1600 + D:1600 + D + FS * B]
        lift = c_arena[:, 0:2 * KD * L].rearrange("p (s k n) -> p s k n", s=2, k=KD)
        mixed = kv_arena[0:L, 0:GB * D].rearrange("p (s n) -> p s n", s=GB)
        final = kv_arena[0:L, GB * D:2 * GB * D].rearrange("p (s n) -> p s n", s=GB)
        squares = kv_arena[0:L, 2 * GB * D:3 * GB * D].rearrange("p (s n) -> p s n", s=GB)
        norm_w, in_gamma, in_beta, gate_b, bc_b = (vecs[:, i, :] for i in range(5))
        pn_gamma, pn_beta = (pn_vecs[:, i, :] for i in range(2))

        ps_s = ctx.enter_context(nc.psum_tensor("ps_s", [P, 2, 512], F32))
        ps_pt = ctx.enter_context(nc.psum_tensor("ps_pt", [P, 2, 512], F32))
        ps_mm = [ctx.enter_context(nc.psum_tensor(f"ps_mm{i}", [P, 512], F32)) for i in range(2)]
        ps_pv = ctx.enter_context(nc.psum_tensor("ps_pv", [P, 512], F32))
        ps_tr = ctx.enter_context(nc.psum_tensor("ps_tr", [P, 512], F32))

        x_first_loaded, x_rest_loaded, ctx_loaded, const_loaded, mask_loaded, mask_row_loaded, row_loaded = (
            sem(n) for n in ("x_first_loaded", "x_rest_loaded", "ctx_loaded", "const_loaded", "mask_loaded",
                             "mask_row_loaded", "row_loaded"))
        w_loaded = {n: sem(f"{n}_loaded") for n in ("wq", "wk", "wg", "wv", "wo", "fg", "agg", "bc", "d1", "d2")}
        last_row_loaded = sem("last_row_loaded")
        stored = [sem(f"stored{s}") for s in range(GB)]
        filled, zeroed, bias_made, flag_step, flag_set, half_made = (
            sem(n) for n in ("filled", "zeroed", "bias_made", "flag_step", "flag_set", "half_made"))
        st_made, mv_made, var_ready, rstd_ready, norm_ready = (
            sem(n) for n in ("st_made", "mv_made", "var_ready", "rstd_ready", "norm_ready"))
        xt_done, xt_kept, back1_done = sem("xt_done"), sem("xt_kept"), sem("back1_done")
        done = {k: sem(f"{k}_done") for k in ("q", "k", "v", "g", "o")}
        kept = {k: sem(f"{k}_kept") for k in ("q", "k", "v", "g", "o")}
        scored, maxed, shifted, raised, summed, inverted, weighted, divided, turned, turn_kept, mixed_v, mix_kept = (
            sem(n) for n in ("scored", "maxed", "shifted", "raised", "summed", "inverted", "weighted", "divided",
                             "turned", "turn_kept", "mixed_v", "mix_kept"))
        x1_ready, st1_made, mv1_made, mean1_ready, var1_ready, rstd1_ready = (
            sem(n) for n in ("x1_ready", "st1_made", "mv1_made", "mean1_ready", "var1_ready", "rstd1_ready"))
        norm2_ready, tr2_done, tr2_used, fg_done, fg_kept = (
            sem(n) for n in ("norm2_ready", "tr2_done", "tr2_used", "fg_done", "fg_kept"))
        th_ready, th_st_made, th_mv_made, th_var_ready, th_rstd_ready, th_normed = (
            sem(n) for n in ("th_ready", "th_st_made", "th_mv_made", "th_var_ready", "th_rstd_ready", "th_normed"))
        (tht_done, tht_scaled, tht_ready, up_done, up_kept, upt_done, z_ready, hid_ready, down_done,
         down_kept, sum_done) = (sem(n) for n in (
             "tht_done", "tht_scaled", "tht_ready", "up_done", "up_kept", "upt_done", "z_ready",
             "hid_ready", "down_done", "down_kept", "sum_done"))
        agg_done, bc_done, bc_ready = sem("agg_done"), sem("bc_done"), sem("bc_ready")
        (lifted, back_done, o_ready, o_minus_ready, o_mean_ready, o_var_ready, o_eps_added, o_rstd_ready,
         o_scaled, x_biased, out_ready) = (sem(n) for n in (
             "lifted", "back_done", "o_ready", "o_minus_ready", "o_mean_ready", "o_var_ready",
             "o_eps_added", "o_rstd_ready", "o_scaled", "x_biased", "out_ready"))

        tail, full = Geometry(False), Geometry(True)

        def each_group(eng, body):
            body(0, False)
            with eng.Fori(1, NG - 1) as g:
                body(g, False)
            body(NG - 1, True)

        def is_first(g):
            return isinstance(g, int) and g == 0

        def each_out(eng, body):
            for s in range(GB):
                body(0, s)
            with eng.Fori(1, NG - 1) as g:
                for s in range(GB):
                    body(g, s)
            for s in range(GB):
                body(NG - 1, s)

        passed = {n: sem(f"{n}_passed") for n in ("pe", "act", "dve", "pool")}

        def wait_apart(name, eng, signal, value):
            eng.wait_ge(signal, value)
            eng.sem_inc(passed[name], 1)

        def branch(eng, tail_part, full_part):
            eng.wait_ge(flag_set, 1)
            seen = eng.value_load(flag[0:1, 0:1], min_val=0, max_val=1)
            with eng.If(seen > 0):
                full_part()
            with eng.Else():
                tail_part()

        block = ctx.enter_context(nc.Block())

        @block.sync
        def _(sp):
            def load_x(first, n, signal):
                sp.dma_start(x[:, first:first + n, :],
                             a["x"][first:first + n].rearrange("b l d -> l b d")).then_inc(signal, 16)

            def load_w(name, dst):
                sp.dma_start(dst, a[name]).then_inc(w_loaded[name], 16)

            def load_ctx(geo, i):
                src = a["ctx_full"] if geo.full else a["ctx_tail"]
                sp.dma_start(ctx_t[:, 0:KD * geo.lot_keys],
                             src[bass.ds(i, 1)].rearrange("a p n -> p (a n)")).then_inc(ctx_loaded, 16)

            def load_mask_row(geo):
                src = a["mask_row_full"] if geo.full else a["mask_row_tail"]
                sp.dma_start(mask_row[:, 0:B * geo.keys], src).then_inc(mask_row_loaded, 16)

            def load_rest():
                load_w("wv", wv)
                load_w("wg", wg)
                load_x(GB, B - GB, x_rest_loaded)
                load_w("wo", wo[:, :, :])
                load_w("agg", agg[:, :, :])
                load_w("fg", fg[:, :, :])
                load_w("bc", bc[:, :, :])
                for dst, name in ((pick, "pick"), (pn_vecs, "pn_vecs"), (d1b, "d1b"), (agg_b, "agg_b"),
                                  (d2_b, "d2_b")):
                    sp.dma_start(dst[:], a[name]).then_inc(row_loaded, 16)
                for dst, name in ((gamma_row, "out_gamma"), (beta_row, "out_beta")):
                    sp.dma_start(dst[:, :], a[name].to_broadcast([L, D])).then_inc(row_loaded, 16)

            sp.dma_start(mask_any[:, :], a["mask"][:, 0:HEAD_ROWS]).then_inc(mask_loaded, 16)
            load_w("wk", wk)
            load_x(0, GB, x_first_loaded)
            sp.dma_start(ident[:, :], a["ident"]).then_inc(const_loaded, 16)
            sp.dma_start(vecs[:, :, :], a["vecs"]).then_inc(const_loaded, 16)

            def attend(geo):
                load_ctx(geo, 0)
                load_w("wq", wq)
                load_mask_row(geo)
                load_rest()
                with sp.Fori(1, NG * geo.lots) as i:
                    sp.wait_ge(done["v"], geo.v_tiles * i)
                    load_ctx(geo, i)
                sp.wait_ge(done["v"], geo.v_tiles * NG * geo.lots)
                sp.wait_ge(done["g"], KD * NG)
                load_w("d1", d1)
                sp.wait_ge(mixed_v, geo.group_units * NG)
                load_w("d2", d2)

            branch(sp, lambda: attend(tail), lambda: attend(full))
            sp.wait_ge(x1_ready, B)
            sp.dma_start(last_row[:, :], x[L - 1:L, :, :]).then_inc(last_row_loaded, 16)
            with sp.Fori(0, NG) as g:
                for s in range(GB):
                    sp.wait_ge(out_ready, GB * g + s + 1)
                    sp.dma_start(a["out"][bass.ds(GB * g + s, 1)].rearrange("b l d -> l (b d)"),
                                 final[:, s, :]).then_inc(stored[s], 16)
            for s in range(GB):
                sp.wait_ge(stored[s], 16 * NG)

        @block.tensor
        def _(pe):
            mm_uses = []

            def project(kind, count, rows, cols, mats, need=()):
                use = len(mm_uses)
                bank = ps_mm[use % 2]
                if use >= 2:
                    kind2, count2 = mm_uses[use - 2]
                    pe.wait_ge(kept[kind2], count2)
                for s, v in need:
                    pe.wait_ge(s, v)
                for k in range(KD):
                    lhs, rhs = mats(k)
                    mm = pe.matmul(bank[0:rows, 0:cols], lhs, rhs, start=(k == 0), stop=(k == KD - 1))
                mm.then_inc(done[kind], 1)
                mm_uses.append((kind, count))

            def turn_x(n, b, after=None):
                if b:
                    pe.wait_ge(xt_kept, GB * n + b)
                elif after is not None:
                    pe.wait_ge(x1_ready, GB * after + GB)
                pe.wait_ge(norm_ready, GB * n + b + 1)
                for k in range(KD):
                    t = pe.transpose(ps_tr[:, k * L:(k + 1) * L], normed[:, b % 2, k * P:(k + 1) * P],
                                     ident[0:L, 0:L])
                t.then_inc(xt_done, 1)

            def project_q(n, m):
                project("q", KD * n + m + 1, P, GL, lambda k: (wq[:, k, m * P:(m + 1) * P], x_t[:, k, :]),
                        [(w_loaded["wq"], 16), (xt_kept, GB * n + GB)])

            def project_g(n, m):
                project("g", KD * n + m + 1, P, GL, lambda k: (wg[:, k, m * P:(m + 1) * P], x_t[:, k, :]),
                        [(w_loaded["wg"], 16), (xt_kept, GB * n + GB)])

            def ctx_cols(geo, k):
                return ctx_t[:, k * geo.lot_keys:(k + 1) * geo.lot_keys]

            def project_k(geo, i, m):
                project("k", KD * i + m + 1, P, geo.lot_keys,
                        lambda k: (wk[:, k, m * P:(m + 1) * P], ctx_cols(geo, k)),
                        [(w_loaded["wk"], 16), (ctx_loaded, 16 * i + 16)])

            def project_v(geo, i, c):
                first, rows = geo.chunks[c] if geo.full else (c * TAIL, TAIL)
                project("v", geo.v_tiles * i + c + 1, rows, D,
                        lambda k: (ctx_cols(geo, k)[:, first:first + rows], wv[:, k, :]),
                        [(w_loaded["wv"], 16), (ctx_loaded, 16 * i + 16)])

            def project_o(g, m):
                project("o", KD * g + m + 1, P, GL, lambda k: (wo[:, k, m * P:(m + 1) * P], att_t[:, k, :]),
                        [(w_loaded["wo"], 16)])

            def scores(geo, g, lot, u):
                unit = geo.group_units * g + geo.units * lot + u
                i = geo.lots * g + lot
                b = geo.batch(lot, u)
                if u == 0:
                    pe.wait_ge(kept["q"], KD * g + KD)
                    pe.wait_ge(kept["k"], KD * i + KD)
                if u or lot:
                    pe.wait_ge(shifted, unit)
                w = geo.bank_heads * geo.keys
                for k in range(2):
                    h0 = geo.heads(u, k)[0]
                    col = (h0 if geo.full else NH * b + h0) * geo.keys
                    bank = ps_s[0:L, k, 0:w]
                    pe.matmul(bank, q_t[:, h0 // 4, b * L:(b + 1) * L], keys[:, col:col + w], start=True, stop=False)
                    bias = mask_bias[:, bass.ds((GB * g + b) * geo.keys, geo.keys)]
                    if geo.bank_heads > 1:
                        bias = bias.unsqueeze(1).to_broadcast([1, geo.bank_heads, geo.keys])
                    mm = pe.matmul(bank, ones_bf[:, 0:L], bias, start=False, stop=True)
                mm.then_inc(scored, 1)

            def turn_probs(geo, g, lot, u):
                unit = geo.group_units * g + geo.units * lot + u
                if u or lot:
                    pe.wait_ge(turn_kept, unit)
                pe.wait_ge(divided, unit + 1)
                for k in range(2):
                    n = 0
                    for j, _ in enumerate(geo.heads(u, k)):
                        for first, rows in geo.chunks:
                            col = (k * geo.bank_heads + j) * geo.keys + first
                            t = pe.transpose(ps_pt[0:rows, k, n * L:(n + 1) * L], probs[u % 2][:, col:col + rows],
                                             ident[0:L, 0:L])
                            n += 1
                t.then_inc(turned, 1)

            def mix_values(geo, g, lot, u):
                unit = geo.group_units * g + geo.units * lot + u
                pe.wait_ge(turn_kept, unit + 1)
                if u or lot:
                    pe.wait_ge(mix_kept, unit)
                i = geo.lots * g + lot
                pe.wait_ge(kept["v"], geo.v_tiles * i + (geo.v_tiles if geo.full else geo.batch(lot, u) + 1))
                n = 0
                for k in range(2):
                    for h in geo.heads(u, k):
                        r = HD * (h % 4)
                        out = ps_pv[r:r + HD, (0 if geo.full else k) * L:((0 if geo.full else k) + 1) * L]
                        for c, (first, rows) in enumerate(geo.chunks):
                            v = values[0:rows, c if geo.full else geo.batch(lot, u), h * HD:(h + 1) * HD]
                            mm = pe.matmul(out, v, probs_t[0:rows, n * L:(n + 1) * L], start=(c == 0),
                                           stop=(c == len(geo.chunks) - 1))
                            n += 1
                mm.then_inc(mixed_v, 1)

            def turn_back(g, b):
                if b:
                    pe.wait_ge(x1_ready, GB * g + b)
                pe.wait_ge(kept["o"], KD * g + KD)
                for k in range(KD):
                    t = pe.transpose(ps_tr[0:L, k * P:(k + 1) * P], gate_t[:, k, b * L:(b + 1) * L], ident[:, :])
                t.then_inc(back1_done, 1)

            def tail_part():
                mm_uses[:] = []
                for m in range(KD):
                    project_k(tail, 0, m)
                for b in range(GB):
                    turn_x(0, b)
                for m in range(KD):
                    project_q(0, m)

                def body(g, last):
                    mm_uses[:] = [("q", KD - 1), ("q", KD)] if is_first(g) else [("o", KD * g - 1), ("o", KD * g)]
                    for u in range(tail.units):
                        scores(tail, g, 0, u)
                        if u >= 2:
                            turn_probs(tail, g, 0, u - 2)
                        if u < GB:
                            project_v(tail, g, u)
                            if not is_first(g):
                                turn_back(g - 1, u)
                        else:
                            project_g(g, u - GB)
                        if u >= 2:
                            mix_values(tail, g, 0, u - 2)
                    n = g + 1
                    if not last:
                        turn_x(n, 0, None if is_first(g) else g - 1)
                        project_k(tail, n, 0)
                        turn_x(n, 1)
                        turn_probs(tail, g, 0, 6)
                        project_k(tail, n, 1)
                        mix_values(tail, g, 0, 6)
                        turn_x(n, 2)
                        project_k(tail, n, 2)
                        turn_x(n, 3)
                        turn_probs(tail, g, 0, 7)
                        project_k(tail, n, 3)
                        mix_values(tail, g, 0, 7)
                        for m in range(KD):
                            project_q(n, m)
                    else:
                        for u in (6, 7):
                            turn_probs(tail, g, 0, u)
                            mix_values(tail, g, 0, u)
                    pe.wait_ge(mix_kept, tail.units * g + tail.units)
                    for m in range(KD):
                        project_o(g, m)
                    if last:
                        pe.wait_ge(x1_ready, GB * g)
                        for b in range(GB):
                            turn_back(g, b)

                pe.wait_ge(bias_made, 1)
                each_group(pe, body)

            def full_part():
                pe.wait_ge(bias_made, 1)
                with pe.Fori(0, NG) as g:
                    mm_uses[:] = []
                    for b in range(GB):
                        turn_x(g, b)
                    for m in range(KD):
                        project_q(g, m)
                    for m in range(KD):
                        project_g(g, m)
                    for lot in range(GB):
                        for m in range(KD):
                            project_k(full, GB * g + lot, m)
                        for c in range(full.v_tiles):
                            project_v(full, GB * g + lot, c)
                        for u in range(full.units):
                            scores(full, g, lot, u)
                            if u >= 2:
                                turn_probs(full, g, lot, u - 2)
                                mix_values(full, g, lot, u - 2)
                        for u in (6, 7):
                            turn_probs(full, g, lot, u)
                            mix_values(full, g, lot, u)
                    pe.wait_ge(mix_kept, full.group_units * g + full.group_units)
                    for m in range(KD):
                        project_o(g, m)
                    for b in range(GB):
                        turn_back(g, b)
                    pe.wait_ge(x1_ready, GB * g + GB)

            pe.wait_ge(const_loaded, 32)
            pe.wait_ge(filled, 5)
            branch(pe, tail_part, full_part)

            def turn_thought(i):
                wait_apart("pe", pe, th_normed, i + 1)
                for k in range(KD):
                    t = pe.transpose(ps_pt[:, 1, k * B:(k + 1) * B], th_norm[:, k * P:(k + 1) * P], ident[0:B, 0:B])
                t.then_inc(tht_done, 1)

            def turn_x2(s, b):
                if b:
                    pe.wait_ge(tr2_used, GB * s + b)
                pe.wait_ge(norm2_ready, GB * s + b + 1)
                for k in range(KD):
                    t = pe.transpose(ps_tr[:, k * L:(k + 1) * L], normed[:, b % 2, k * P:(k + 1) * P],
                                     ident[0:L, 0:L])
                t.then_inc(tr2_done, 1)

            def gate(s, m):
                if m >= 2:
                    pe.wait_ge(fg_kept, KD * s + m - 1)
                pe.wait_ge(tr2_used, GB * s + GB)
                for k in range(KD):
                    mm = pe.matmul(ps_mm[m % 2][:, 0:GL], fg[:, k, m * P:(m + 1) * P], x2_t[:, k, :],
                                   start=(k == 0), stop=(k == KD - 1))
                mm.then_inc(fg_done, 1)

            def think(s, gates):
                n = s + 1
                if gates:
                    turn_x2(n, 0)
                    turn_x2(n, 1)
                turn_thought(s + 1)
                if gates:
                    turn_x2(n, 2)
                pe.wait_ge(tht_ready, s + 2)
                for k in range(KD):
                    for j in range(FJ):
                        mm = pe.matmul(ps_s[32 * j:32 * j + 32, 0, :], th_t[:, k, :], d1[:, k, j * D:(j + 1) * D],
                                       start=(k == 0), stop=(k == KD - 1))
                mm.then_inc(up_done, 1)
                if gates:
                    turn_x2(n, 3)
                pe.wait_ge(up_kept, s + 1)
                for i in range(KD):
                    t = pe.transpose(ps_pt[:, 0, i * P:(i + 1) * P], hid[:, i * P:(i + 1) * P], ident[:, :])
                t.then_inc(upt_done, 1)
                if gates:
                    gate(n, 0)
                pe.wait_ge(hid_ready, s + 1)
                for i in range(KD):
                    for j in range(FJ):
                        mm = pe.matmul(ps_s[32 * j:32 * j + 32, 1, :], hid_t[:, KD * i + j, :], d2[:, KD * j + i, :],
                                       start=(i == 0), stop=(i == KD - 1))
                mm.then_inc(down_done, 1)
                if gates:
                    gate(n, 1)
                pe.matmul(ps_pv[0:B, :], ones[:, :], d2_b[:, :], start=True, stop=False)
                pe.wait_ge(down_kept, s + 1)
                pe.matmul(ps_pv[0:B, :], pick[:, :], parts, start=False, stop=True).then_inc(sum_done, 1)
                if gates:
                    gate(n, 2)
                    gate(n, 3)

            pe.wait_ge(w_loaded["fg"], 16)
            for b in range(GB):
                turn_x2(0, b)
            gate(0, 0)
            gate(0, 1)
            turn_thought(0)
            gate(0, 2)
            pe.wait_ge(w_loaded["agg"], 16)
            pe.wait_ge(row_loaded, 16 * 7)
            pe.wait_ge(tht_ready, 1)
            for k in range(KD):
                pe.matmul(ps_pv[0:B, :], th_t[:, k, 0:B], agg[:, k, :], start=(k == 0), stop=False)
            pe.matmul(ps_pv[0:B, :], ones[:, :], agg_b[:, :], start=False, stop=True).then_inc(agg_done, 1)
            gate(0, 3)
            pe.wait_ge(w_loaded["d1"], 16)
            pe.wait_ge(w_loaded["d2"], 16)
            with pe.Fori(0, STEPS - 1) as s:
                think(s, True)
            think(STEPS - 1, False)
            pe.wait_ge(th_ready, STEPS + 1)
            for k in range(KD):
                t = pe.transpose(ps_pt[:, 1, k * B:(k + 1) * B], thought[:, k * P:(k + 1) * P], ident[0:B, 0:B])
            t.then_inc(tht_done, 1)
            pe.wait_ge(w_loaded["bc"], 16)
            pe.wait_ge(tht_ready, STEPS + 2)
            for m in range(KD):
                for k in range(KD):
                    mm = pe.matmul(ps_pv[:, m * B:(m + 1) * B], bc[:, k, m * P:(m + 1) * P], th_t[:, k, 0:B],
                                   start=(k == 0), stop=(k == KD - 1))
            mm.then_inc(bc_done, 1)

            def back(g, s):
                i = GB * g + s
                pe.wait_ge(lifted, i + 1)
                if s >= 2 or not isinstance(g, int) or g:
                    pe.wait_ge(o_ready, i - 1)
                for k in range(KD):
                    t = pe.transpose(ps_mm[s % 2][0:L, k * P:(k + 1) * P], lift[:, s % 2, k, :], ident[:, :])
                t.then_inc(back_done, 1)

            each_out(pe, back)

        @block.scalar
        def _(act):
            def keep_q(n, m):
                act.wait_ge(done["q"], KD * n + m + 1)
                act.activation(q_t[:, m, :], ps_mm[m % 2][:, 0:GL], ACT.Copy).then_inc(kept["q"], 1)

            def keep_g(n, m):
                act.wait_ge(done["g"], KD * n + m + 1)
                act.activation(gate_t[:, m, :], ps_mm[m % 2][:, 0:GL], ACT.Tanh, scale=0.5).then_inc(kept["g"], 1)

            def keep_k(geo, i, m, bank):
                act.wait_ge(done["k"], KD * i + m + 1)
                for j in range(4):
                    r = slice(HD * j, HD * j + HD)
                    if geo.full:
                        dst = keys[r, (4 * m + j) * M:(4 * m + j + 1) * M]
                        src = bank[r, 0:M]
                    else:
                        dst = keys[r, 0:GB * NH * TAIL].rearrange("p (b h n) -> p b h n", b=GB, h=NH)[:, :, 4 * m + j, :]
                        src = bank[r, 0:GB * TAIL].rearrange("p (b n) -> p b n", b=GB)
                    c = act.activation(dst, src, ACT.Copy)
                c.then_inc(kept["k"], 1)

            def raise_(geo, g, lot, u):
                unit = geo.group_units * g + geo.units * lot + u
                act.wait_ge(shifted, unit + 1)
                w = geo.unit_heads * geo.keys
                act.activation(probs[u % 2][:, 0:w], probs[u % 2][:, 0:w], ACT.Exp, scale=SCALE).then_inc(raised, 1)

            def keep_turned(geo, g, lot, u):
                unit = geo.group_units * g + geo.units * lot + u
                act.wait_ge(turned, unit + 1)
                if geo.full:
                    whole = [c for c in geo.chunks if c[1] == P]
                    w, rest = len(whole) * L, geo.chunks[-1][1]
                    dst = probs_t[:, 0:6 * L].rearrange("p (k n) -> p k n", k=2)
                    act.activation(dst[:, :, 0:w], ps_pt[:, :, 0:w], ACT.Copy)
                    act.activation(dst[0:rest, :, w:w + L], ps_pt[0:rest, :, w:w + L], ACT.Copy).then_inc(turn_kept, 1)
                else:
                    dst = probs_t[0:TAIL, :].rearrange("p (k n) -> p k n", k=2)
                    act.activation(dst, ps_pt[0:TAIL, :, 0:4 * L], ACT.Copy).then_inc(turn_kept, 1)

            def keep_mixed(geo, g, lot, u):
                unit = geo.group_units * g + geo.units * lot + u
                b = geo.batch(lot, u)
                act.wait_ge(mixed_v, unit + 1)
                if geo.full:
                    r = slice(64 * (u % 2), 64 * (u % 2) + 64)
                    dst, src = att_t[r, u // 2, b * L:(b + 1) * L], ps_pv[r, 0:L]
                else:
                    t = 2 * (u % 2)
                    dst = att_t[:, t:t + 2, b * L:(b + 1) * L]
                    src = ps_pv[:, 0:2 * L].rearrange("p (k n) -> p k n", k=2)
                act.activation(dst, src, ACT.Copy).then_inc(mix_kept, 1)

            def tail_part():
                act.wait_ge(zeroed, 1)
                for m in range(KD):
                    keep_k(tail, 0, m, ps_mm[m % 2])
                for m in range(KD):
                    keep_q(0, m)

                def body(g, last):
                    for u in range(tail.units):
                        if u >= 2:
                            keep_turned(tail, g, 0, u - 2)
                        raise_(tail, g, 0, u)
                        if u >= GB:
                            keep_g(g, u - GB)
                        if u >= 2:
                            keep_mixed(tail, g, 0, u - 2)
                    n = g + 1
                    if not last:
                        keep_k(tail, n, 0, ps_mm[0])
                    keep_turned(tail, g, 0, 6)
                    if not last:
                        keep_k(tail, n, 1, ps_mm[1])
                    keep_mixed(tail, g, 0, 6)
                    if not last:
                        keep_k(tail, n, 2, ps_mm[0])
                    keep_turned(tail, g, 0, 7)
                    if not last:
                        keep_k(tail, n, 3, ps_mm[1])
                    keep_mixed(tail, g, 0, 7)
                    if not last:
                        for m in range(KD):
                            keep_q(n, m)

                each_group(act, body)

            def full_part():
                act.wait_ge(zeroed, 1)
                with act.Fori(0, NG) as g:
                    for m in range(KD):
                        keep_q(g, m)
                    for m in range(KD):
                        keep_g(g, m)
                    uses = 2 * KD
                    for lot in range(GB):
                        for m in range(KD):
                            keep_k(full, GB * g + lot, m, ps_mm[(uses + m) % 2])
                        uses += KD + full.v_tiles
                        for u in range(full.units):
                            raise_(full, g, lot, u)
                            if u >= 2:
                                keep_turned(full, g, lot, u - 2)
                                keep_mixed(full, g, lot, u - 2)
                        for u in (6, 7):
                            keep_turned(full, g, lot, u)
                            keep_mixed(full, g, lot, u)

            branch(act, tail_part, full_part)

            def keep_x2(s, b):
                act.wait_ge(tr2_done, GB * s + b + 1)
                act.activation(x2_t[:, :, b * L:(b + 1) * L],
                               ps_tr[:, 0:GL].rearrange("p (k n) -> p k n", k=KD), ACT.Copy).then_inc(tr2_used, 1)

            def keep_gate(s, m):
                act.wait_ge(fg_done, KD * s + m + 1)
                act.activation(gates[:, m, bass.ds(s * GL, GL)], ps_mm[m % 2][:, 0:GL], ACT.Tanh,
                               bias=half_gate_b[:, m:m + 1], scale=0.5).then_inc(fg_kept, 1)

            act.wait_ge(half_made, 1)
            for b in range(GB):
                keep_x2(0, b)
            for m in range(KD):
                keep_gate(0, m)

            def think(s, gates):
                if gates:
                    keep_x2(s + 1, 0)
                    keep_x2(s + 1, 1)
                    keep_x2(s + 1, 2)
                act.wait_ge(up_done, s + 1)
                act.activation(hid, ps_s[:, 0, :], ACT.Copy).then_inc(up_kept, 1)
                if gates:
                    keep_x2(s + 1, 3)
                act.wait_ge(z_ready, s + 1)
                act.activation(hid_t[:, :, 0:B], z_t.rearrange("p (f b) -> p f b", f=FS),
                               ACT.Gelu).then_inc(hid_ready, 1)
                if gates:
                    keep_gate(s + 1, 0)
                act.wait_ge(down_done, s + 1)
                act.activation(parts, ps_s[:, 1, :], ACT.Copy).then_inc(down_kept, 1)
                if gates:
                    for m in range(1, KD):
                        keep_gate(s + 1, m)

            with act.Fori(0, STEPS - 1) as s:
                think(s, True)
            think(STEPS - 1, False)

            def raise_gate(g, s):
                i = GB * g + s
                if not (is_first(g) and s < 2):
                    act.wait_ge(back_done, i - 1)
                for k in range(KD):
                    row = bc_half[:, k, bass.ds(i, 1)]
                    c = act.activation(lift[:, s % 2, k, :], gates[:, k, bass.ds(i * L, L)], ACT.Identity, bias=row,
                                       scale=row)
                c.then_inc(lifted, 1)

            def measure_out(g, s):
                i = GB * g + s
                if not (isinstance(g, int) and i == NG * GB - 1):
                    raise_gate(g + (s + 1) // GB, (s + 1) % GB)
                act.wait_ge(o_mean_ready, i + 1)
                act.activation(squares[:, s, :], mixed[:, s, :], ACT.Square, bias=o_mean[:, s:s + 1],
                               scale=float(D) ** -0.5, accum_out=o_var[:, s:s + 1]).then_inc(o_var_ready, 1)

            act.wait_ge(bc_ready, KD)
            raise_gate(0, 0)
            each_out(act, measure_out)

        @block.vector
        def _(dve):
            dve.memset(flag_a[:, :], 0.0).then_inc(flag_step, 1)
            dve.wait_ge(flag_step, 1)
            dve.wait_ge(mask_loaded, 16)
            dve.tensor_reduce(flag_a[0:B, 0:1], mask_any[:, :], AX_X, ALU.max).then_inc(flag_step, 1)
            dve.wait_ge(flag_step, 2)
            dve.transpose(flag_b[:, :], flag_a[:, :]).then_inc(flag_step, 1)
            dve.wait_ge(flag_step, 3)
            dve.tensor_reduce(flag[0:1, 0:1], flag_b[0:1, :], AX_X, ALU.max).then_inc(flag_set, 1)

            def statistics(g, b):
                if isinstance(g, int) and g == 0:
                    dve.wait_ge(x_first_loaded, 16)
                else:
                    dve.wait_ge(x_rest_loaded, 16)
                dve.bn_stats(st[:, b, :], x[:, bass.ds(GB * g + b, 1), :].rearrange("p a n -> p (a n)")
                             ).then_inc(st_made, 1)
                wait_apart("dve", dve, st_made, GB * g + b + 1)
                dve.bn_aggr(mv[:, b, :], st[:, b, :]).then_inc(mv_made, 1)

            def variance(g):
                dve.wait_ge(mv_made, GB * g + GB)
                dve.tensor_scalar(vr[:, :].unsqueeze(2), mv[:, :, 1:2],
                                  1.0 + EPS_IN, EPS_LN * EPS_IN, ALU.mult, ALU.add).then_inc(var_ready, 1)

            def normalise(g, b):
                if b >= 2:
                    dve.wait_ge(xt_done, GB * g + b - 1)
                if b == 0:
                    dve.wait_ge(rstd_ready, g + 1)
                i = GB * g + b
                dve.tensor_scalar(normed[:, b % 2, :], x[:, bass.ds(i, 1), :].rearrange("p a n -> p (a n)"),
                                  mv[:, b, 0:1], rstd[:, b:b + 1],
                                  ALU.subtract, ALU.mult).then_inc(norm_ready, 1)

            def keep_x(g, b):
                dve.wait_ge(xt_done, GB * g + b + 1)
                dve.tensor_tensor(x_t[:, :, b * L:(b + 1) * L], ps_tr[:, 0:GL].rearrange("p (k n) -> p k n", k=KD),
                                  norm_w.unsqueeze(2).to_broadcast([P, KD, L]), ALU.mult).then_inc(xt_kept, 1)

            def turn_group(g):
                for b in range(GB):
                    normalise(g, b)
                    if b >= 1:
                        keep_x(g, b - 1)
                keep_x(g, GB - 1)

            def make_bias(geo):
                n = B * geo.keys
                dve.wait_ge(mask_row_loaded, 16)
                dve.tensor_scalar(mask_bias[:, 0:n], mask_row[:, 0:n], -MASKED, MASKED, ALU.mult,
                                  ALU.add).then_inc(bias_made, 1)

            def scores_view(geo):
                return ps_s[0:L, :, 0:geo.bank_heads * geo.keys].rearrange("p k (h n) -> p k h n", h=geo.bank_heads)

            def probs_view(geo, u):
                return probs[u % 2][:, 0:geo.unit_heads * geo.keys].rearrange(
                    "p (k h n) -> p k h n", k=2, h=geo.bank_heads)

            def per_head(t, geo, u):
                return t[:, u % 2, 0:geo.unit_heads]

            def subtract_max(geo, g, lot, u):
                unit = geo.group_units * g + geo.units * lot + u
                dve.wait_ge(scored, unit + 1)
                if u >= 2 or lot:
                    dve.wait_ge(weighted, unit - 1)
                mx = per_head(row_max, geo, u)
                mx4 = mx.rearrange("p (k h) -> p k h", k=2)
                dve.tensor_reduce(mx4, scores_view(geo), AX_X, ALU.max).then_inc(maxed, 1)
                dve.wait_ge(maxed, unit + 1)
                if u >= 2 or lot:
                    dve.wait_ge(turned, unit - 1)
                dve.tensor_tensor(probs_view(geo, u), scores_view(geo),
                                  mx4.unsqueeze(3).to_broadcast([L, 2, geo.bank_heads, geo.keys]),
                                  ALU.subtract).then_inc(shifted, 1)

            def invert_sum(geo, g, lot, u):
                unit = geo.group_units * g + geo.units * lot + u
                dve.wait_ge(raised, unit + 1)
                sm, inv, mx = (per_head(t, geo, u) for t in (row_sum, row_inv, row_max))
                dve.tensor_reduce(sm.rearrange("p (k h) -> p k h", k=2), probs_view(geo, u), AX_X,
                                  ALU.add).then_inc(summed, 1)
                dve.wait_ge(summed, unit + 1)
                dve.reciprocal(inv, sm).then_inc(inverted, 1)
                dve.wait_ge(inverted, unit + 1)
                dve.scalar_tensor_tensor(out=inv, in0=mx, scalar=ALIVE, in1=inv, op0=ALU.is_gt,
                                         op1=ALU.mult).then_inc(weighted, 1)

            def keep_v(geo, i, c, bank):
                rows = geo.chunks[c][1] if geo.full else TAIL
                dve.wait_ge(done["v"], geo.v_tiles * i + c + 1)
                dve.tensor_copy(values[0:rows, c, :], bank[0:rows, :]).then_inc(kept["v"], 1)

            def gate_output(g, m):
                dve.wait_ge(done["o"], KD * g + m + 1)
                if m == 0:
                    dve.wait_ge(kept["g"], KD * g + KD)
                dve.scalar_tensor_tensor(out=gate_t[:, m, :], in0=gate_t[:, m, :], scalar=1.0,
                                         in1=ps_mm[m % 2][:, 0:GL], op0=ALU.add, op1=ALU.mult).then_inc(kept["o"], 1)

            def add_attention(g, b):
                i = GB * g + b
                dve.wait_ge(back1_done, i + 1)
                row = x[:, bass.ds(i, 1), :].rearrange("p a n -> p (a n)")
                dve.scalar_tensor_tensor(out=row, in0=ps_tr[0:L, :], scalar=0.5, in1=row, op0=ALU.mult,
                                         op1=ALU.add).then_inc(x1_ready, 1)
                wait_apart("dve", dve, x1_ready, i + 1)
                dve.bn_stats(st1[:, b, :], row).then_inc(st1_made, 1)
                wait_apart("dve", dve, st1_made, i + 1)
                dve.bn_aggr(mv1[:, b, :], st1[:, b, :]).then_inc(mv1_made, 1)
                if b == GB - 1:
                    dve.wait_ge(mv1_made, i + 1)
                    dve.tensor_copy(mean1[:, bass.ds(GB * g, GB)].unsqueeze(2), mv1[:, :, 0:1]
                                    ).then_inc(mean1_ready, 1)
                    dve.tensor_scalar(vr1[:, bass.ds(GB * g, GB)].unsqueeze(2), mv1[:, :, 1:2],
                                      EPS_LN, None, ALU.add).then_inc(var1_ready, 1)

            for b in range(GB):
                statistics(0, b)
            variance(0)
            dve.wait_ge(const_loaded, 32)

            def tail_part():
                make_bias(tail)
                turn_group(0)

                def body(g, last):
                    n = g + 1
                    for u in range(tail.units):
                        subtract_max(tail, g, 0, u)
                        if u >= 1:
                            invert_sum(tail, g, 0, u - 1)
                        if u < GB:
                            keep_v(tail, g, u, ps_mm[u % 2])
                            if not is_first(g):
                                add_attention(g - 1, u)
                        if GB - 1 <= u < tail.units - 1 and not last:
                            statistics(n, u - GB + 1)
                        if u == tail.units - 2 and not last:
                            variance(n)
                    if not last:
                        normalise(n, 0)
                        normalise(n, 1)
                        keep_x(n, 0)
                    invert_sum(tail, g, 0, 7)
                    if not last:
                        normalise(n, 2)
                        keep_x(n, 1)
                        normalise(n, 3)
                        keep_x(n, 2)
                        keep_x(n, 3)
                    for m in range(KD):
                        gate_output(g, m)
                    if last:
                        for b in range(GB):
                            add_attention(g, b)

                each_group(dve, body)

            def full_part():
                make_bias(full)

                def body(g, last):
                    turn_group(g)
                    uses = 2 * KD
                    for lot in range(GB):
                        uses += KD
                        for c in range(full.v_tiles):
                            keep_v(full, GB * g + lot, c, ps_mm[(uses + c) % 2])
                        uses += full.v_tiles
                        for u in range(full.units):
                            subtract_max(full, g, lot, u)
                            if u >= 1:
                                invert_sum(full, g, lot, u - 1)
                        invert_sum(full, g, lot, 7)
                    for m in range(KD):
                        gate_output(g, m)
                    for b in range(GB):
                        add_attention(g, b)
                    if not last:
                        for b in range(GB):
                            statistics(g + 1, b)
                        variance(g + 1)

                each_group(dve, body)

            branch(dve, tail_part, full_part)

            def measure(src, i, scale, eps):
                dve.bn_stats(th_st[:, :], src).then_inc(th_st_made, 1)
                wait_apart("dve", dve, th_st_made, i + 1)
                dve.bn_aggr(th_mv[:, :], th_st[:, :]).then_inc(th_mv_made, 1)
                dve.wait_ge(th_mv_made, i + 1)
                dve.tensor_scalar(th_var[:, :], th_mv[:, 1:2], scale, eps, ALU.mult, ALU.add).then_inc(th_var_ready, 1)

            def normalise_thought(src, i):
                dve.wait_ge(th_rstd_ready, i + 1)
                dve.tensor_scalar(th_norm[:, :], src, th_mv[:, 0:1], th_rstd[:, 0:1], ALU.subtract,
                                  ALU.mult).then_inc(th_normed, 1)

            def scale_thought(i, gamma, beta):
                dve.wait_ge(tht_done, i + 1)
                dve.tensor_tensor(th_t0[:, :, :], ps_pt[:, 1, 0:KD * B].rearrange("p (k n) -> p k n", k=KD),
                                  gamma.unsqueeze(2).to_broadcast([P, KD, B]), ALU.mult).then_inc(tht_scaled, 1)
                dve.wait_ge(tht_scaled, i + 1)
                dve.tensor_tensor(th_t[:, :, 0:B], th_t0[:, :, :], beta.unsqueeze(2).to_broadcast([P, KD, B]),
                                  ALU.add).then_inc(tht_ready, 1)

            def normalise2(s, b):
                if b >= 2:
                    dve.wait_ge(tr2_done, GB * s + b - 1)
                if b == 0:
                    dve.wait_ge(rstd1_ready, s + 1)
                i = GB * s + b
                dve.tensor_scalar(normed[:, b % 2, :], x[:, bass.ds(i, 1), :].rearrange("p a n -> p (a n)"),
                                  mean1[:, bass.ds(i, 1)], rstd1[:, bass.ds(i, 1)],
                                  ALU.subtract, ALU.mult).then_inc(norm2_ready, 1)

            for b in range(GB):
                normalise2(0, b)
            dve.wait_ge(last_row_loaded, 16)
            measure(last_row[:, :], 0, 1.0 + EPS_IN, EPS_LN * EPS_IN)
            normalise_thought(last_row[:, :], 0)
            dve.wait_ge(filled, 5)
            dve.wait_ge(row_loaded, 16 * 7)
            scale_thought(0, in_gamma, in_beta)
            dve.wait_ge(agg_done, 1)
            dve.tensor_copy(thought[:, :], ps_pv[0:B, :]).then_inc(th_ready, 1)

            def think(s, gates):
                wait_apart("dve", dve, th_ready, s + 1)
                measure(thought[:, :], s + 1, 1.0, EPS_IN)
                if gates:
                    normalise2(s + 1, 0)
                    normalise2(s + 1, 1)
                normalise_thought(thought[:, :], s + 1)
                if gates:
                    normalise2(s + 1, 2)
                scale_thought(s + 1, pn_gamma, pn_beta)
                if gates:
                    normalise2(s + 1, 3)
                dve.wait_ge(upt_done, s + 1)
                dve.tensor_tensor(z_t.rearrange("p (i j b) -> p i j b", i=KD, j=FJ),
                                  ps_pt[:, 0, :].rearrange("p (i j b) -> p i j b", i=KD, j=FJ)[:, :, :, 0:B],
                                  d1b[:, :, :].unsqueeze(3).to_broadcast([P, KD, FJ, B]), ALU.add).then_inc(z_ready, 1)
                dve.wait_ge(sum_done, s + 1)
                dve.tensor_tensor(thought[:, :], ps_pv[0:B, :], thought[:, :], ALU.add).then_inc(th_ready, 1)

            with dve.Fori(0, STEPS - 1) as s:
                think(s, True)
            think(STEPS - 1, False)
            dve.wait_ge(tht_done, STEPS + 2)
            dve.tensor_copy(th_t[:, :, 0:B], ps_pt[:, 1, 0:KD * B].rearrange("p (k n) -> p k n", k=KD)
                            ).then_inc(tht_ready, 1)
            dve.wait_ge(bc_done, 1)
            for m in range(KD):
                dve.tensor_scalar(bc_half[:, m, :], ps_pv[:, m * B:(m + 1) * B], bc_b[:, m:m + 1], 0.5, ALU.add,
                                  ALU.mult).then_inc(bc_ready, 1)
            dve.wait_ge(bc_ready, KD)
            dve.wait_ge(fg_kept, KD * NG)

            def finish(g, s):
                i = GB * g + s
                dve.wait_ge(o_rstd_ready, i + 1)
                dve.wait_ge(o_scaled, i + 1)
                dve.scalar_tensor_tensor(out=final[:, s, :], in0=final[:, s, :], scalar=o_rstd[:, s:s + 1],
                                         in1=x[:, bass.ds(i, 1), :].rearrange("p a n -> p (a n)"), op0=ALU.mult,
                                         op1=ALU.add).then_inc(out_ready, 1)

            def output(g, s):
                i = GB * g + s
                dve.wait_ge(back_done, i + 1)
                dve.scalar_tensor_tensor(out=mixed[:, s, :], in0=x[:, bass.ds(i, 1), :].rearrange("p a n -> p (a n)"),
                                         scalar=rstd1[:, bass.ds(i, 1)], in1=ps_mm[s % 2][0:L, :], op0=ALU.mult,
                                         op1=ALU.add, accum_out=o_sum[:, s:s + 1]).then_inc(o_ready, 1)
                if not (is_first(g) and s < 2):
                    finish(g if s >= 2 else g - 1, (s - 2) % GB)
                dve.wait_ge(o_ready, i + 1)
                dve.tensor_scalar(o_minus[:, s:s + 1], o_sum[:, s:s + 1], -1.0 / D, None, ALU.mult
                                  ).then_inc(o_minus_ready, 1)
                dve.tensor_scalar(o_mean[:, s:s + 1], o_sum[:, s:s + 1], -float(D) ** -1.5, None, ALU.mult
                                  ).then_inc(o_mean_ready, 1)
                if not is_first(g):
                    dve.wait_ge(stored[s], 16 * g)
                dve.wait_ge(o_minus_ready, i + 1)
                dve.scalar_tensor_tensor(out=final[:, s, :], in0=mixed[:, s, :], scalar=o_minus[:, s:s + 1],
                                         in1=gamma_row[:, :], op0=ALU.add, op1=ALU.mult).then_inc(o_scaled, 1)

            each_out(dve, output)
            finish(NG - 1, GB - 2)
            finish(NG - 1, GB - 1)

        @block.gpsimd
        def _(pool):
            for dst, v in ((ones_bf, 1.0), (ones, 1.0), (minus_half, -0.5), (th_t, 0.0), (hid_t, 0.0)):
                pool.memset(dst[:], v).then_inc(filled, 1)
            pool.wait_ge(filled, 5)

            def rstd_of(g):
                pool.wait_ge(var_ready, g + 1)
                pool.tensor_tensor(rstd[:, :], vr[:, :], minus_half[:, 0:GB], ALU.pow).then_inc(rstd_ready, 1)

            def rstd1_of(g):
                pool.wait_ge(var1_ready, g + 1)
                pool.tensor_tensor(rstd1[:, bass.ds(GB * g, GB)], vr1[:, bass.ds(GB * g, GB)], minus_half[:, 0:GB],
                                   ALU.pow).then_inc(rstd1_ready, 1)

            def divide(geo, g, lot, u):
                unit = geo.group_units * g + geo.units * lot + u
                pool.wait_ge(weighted, unit + 1)
                w = probs[u % 2][:, 0:geo.unit_heads * geo.keys].rearrange("p (h n) -> p h n", h=geo.unit_heads)
                inv = row_inv[:, u % 2, 0:geo.unit_heads].unsqueeze(2).to_broadcast([L, geo.unit_heads, geo.keys])
                pool.tensor_tensor(w, w, inv, ALU.mult).then_inc(divided, 1)

            pool.memset(keys, 0.0).then_inc(zeroed, 1)
            rstd_of(0)
            pool.wait_ge(const_loaded, 32)
            pool.tensor_scalar(half_gate_b[:, :], gate_b, 0.5, None, ALU.mult).then_inc(half_made, 1)

            def tail_part():
                def body(g, last):
                    for u in range(tail.units):
                        if u == tail.units - 2 and not last:
                            rstd_of(g + 1)
                        divide(tail, g, 0, u)
                        if u == GB - 1 and not is_first(g):
                            rstd1_of(g - 1)
                    if last:
                        rstd1_of(g)

                each_group(pool, body)

            def full_part():
                def body(g, last):
                    for lot in range(GB):
                        for u in range(full.units):
                            divide(full, g, lot, u)
                    rstd1_of(g)
                    if not last:
                        rstd_of(g + 1)

                each_group(pool, body)

            branch(pool, tail_part, full_part)

            def thought_rstd(i):
                pool.wait_ge(th_var_ready, i + 1)
                pool.tensor_tensor(th_rstd[:, :], th_var[:, :], minus_half[0:B, 0:1], ALU.pow).then_inc(th_rstd_ready, 1)

            thought_rstd(0)
            with pool.Fori(0, STEPS) as s:
                thought_rstd(s + 1)
            pool.wait_ge(row_loaded, 16 * 7)

            def out_stage(g, s):
                i = GB * g + s
                row = x[:, bass.ds(i, 1), :].rearrange("p a n -> p (a n)")
                wait_apart("pool", pool, o_ready, i + 1)
                pool.tensor_tensor(row, row, beta_row[:, :], ALU.add).then_inc(x_biased, 1)
                wait_apart("pool", pool, o_var_ready, i + 1)
                pool.tensor_scalar(o_var_eps[:, s:s + 1], o_var[:, s:s + 1], EPS_IN, None, ALU.add
                                   ).then_inc(o_eps_added, 1)
                pool.wait_ge(o_eps_added, i + 1)
                pool.tensor_tensor(o_rstd[:, s:s + 1], o_var_eps[:, s:s + 1], minus_half[:, 0:1],
                                   ALU.pow).then_inc(o_rstd_ready, 1)

            each_out(pool, out_stage)


def kernel(**inputs):
    import numpy as np
    import concourse.bacc as bacc
    from concourse.bass_utils import run_bass_kernel_spmd

    def arr(name):
        return np.asarray(inputs[name])

    def sliced(w):
        return w.reshape(-1, P, w.shape[-1]).transpose(1, 0, 2)

    def per_partition(v):
        return v.reshape(-1, P).T

    ffn = "L0_ffn_"
    ctx, mask = arr("ctx_2048"), arr("mask_BxS2_bk0")
    ctx_t = ctx.transpose(2, 0, 1).reshape(KD, P, B, M)
    last = ctx_t[:, :, :, HEAD_ROWS:].reshape(KD, P, NG, GB, TAIL)
    arrays = {
        "x": arr("x"),
        "ctx_tail": last.transpose(2, 1, 0, 3, 4).reshape(NG, P, KD * GB * TAIL),
        "ctx_full": ctx_t.transpose(2, 1, 0, 3).reshape(B, P, KD * M),
        "mask": mask,
        "mask_row_tail": mask[:, HEAD_ROWS:].reshape(1, B * TAIL),
        "mask_row_full": mask.reshape(1, B * M),
        "wq": sliced(arr("L0_xattn_wq").T), "wk": sliced(arr("L0_xattn_wk").T),
        "wv": sliced(arr("L0_xattn_wv").T), "wo": sliced(arr("L0_xattn_wo").T),
        "wg": sliced(arr("L0_xattn_wg").T), "fg": sliced(arr(ffn + "gate_w")),
        "agg": sliced(arr(ffn + "agg_w")), "bc": sliced(arr(ffn + "bc_w")),
        "d1": sliced(arr(ffn + "d1_w")), "d2": sliced(arr(ffn + "d2_w")),
        "vecs": np.stack([per_partition(arr(n)) for n in (
            "L0_xattn_norm_w", ffn + "in_gamma", ffn + "in_beta", ffn + "gate_b", ffn + "bc_b")], axis=1),
        "pn_vecs": np.stack([per_partition(arr(ffn + n)) for n in ("pn_gamma", "pn_beta")], axis=1),
        "d1b": arr(ffn + "d1_b").reshape(FJ, KD, P).transpose(2, 1, 0),
        "agg_b": arr(ffn + "agg_b")[None], "d2_b": arr(ffn + "d2_b")[None],
        "out_gamma": arr(ffn + "out_gamma")[None], "out_beta": arr(ffn + "out_beta")[None],
        "ident": np.eye(P, dtype=np.float32),
        "pick": np.array([[float(r % 32 == b) for b in range(B)] for r in range(P)], np.float32),
    }
    nc = bacc.Bacc("TRN2", target_bir_lowering=False, num_devices=1)
    feeds, a = {}, {}
    for name, v in arrays.items():
        v = np.ascontiguousarray(v)
        feeds[f"in_{name}"] = v
        a[name] = nc.dram_tensor(f"in_{name}", v.shape, mybir.dt.from_np(v.dtype), kind="ExternalInput").ap()
    a["out"] = nc.dram_tensor("out_0", (B, L, D), F32, kind="ExternalOutput").ap()
    xattn_ffn(nc, a)
    r = run_bass_kernel_spmd(nc, [feeds], core_ids=[0])
    return r.results[0]["out_0"]
```

```python
from contextlib import ExitStack

import concourse.bass as bass
from concourse import mybir

F32 = mybir.dt.float32
F32R = mybir.dt.float32r
BF16 = mybir.dt.bfloat16
I32 = mybir.dt.int32
ALU = mybir.AluOpType
ACT = mybir.ActivationFunctionType
AX_X = mybir.AxisListType.X

B, L, D, M = 16, 100, 512, 361
NH, HD = 16, 32
P = 128
KD = D // P
GB = 4
NG = B // GB
GL = GB * L
F = 2048
FJ = F // D
FS = F // P
STEPS = 4
TAIL = M // 4
HEAD_ROWS = M - TAIL
SCALE = float(HD) ** -0.5
EPS_LN, EPS_IN = 1e-5, 1e-6
MASKED = -1e30
ALIVE = -5e29


class Geometry:

    def __init__(self, full):
        self.full = full
        self.keys = M if full else TAIL
        self.bank_heads = 1 if full else KD
        self.unit_heads = 2 * self.bank_heads
        self.units = 8
        self.lots = GB if full else 1
        self.group_units = self.units * self.lots
        self.lot_keys = self.keys * (1 if full else GB)
        self.chunks = [(c, min(P, self.keys - c)) for c in range(0, self.keys, P)]
        self.v_tiles = len(self.chunks) if full else GB

    def batch(self, lot, u):
        return lot if self.full else u // 2

    def heads(self, u, k):
        if self.full:
            return [2 * u + k]
        first = 8 * (u % 2) + 4 * k
        return list(range(first, first + 4))


def xattn_ffn(nc, a):
    ctx = ExitStack()
    with ctx:
        def sb(name, shape, dt=F32):
            return ctx.enter_context(nc.sbuf_tensor(name, shape, dt))

        def sem(name):
            return ctx.enter_context(nc.semaphore(name))

        def parts_at(names, at):
            out = []
            for name, n in names:
                out.append(nc.alloc_sbuf_tensor_at(name, [P, KD, n], F32R, offset=at, align_bytes=32))
                at += KD * n * 4
            return out

        x = sb("x", [L, B, D])
        at_w = nc.sbuf_base
        w_arena = sb("w_arena", [P, 4 * KD * D])
        at_o = nc.sbuf_base
        o_arena = sb("o_arena", [P, 2 * KD * D])
        at_kv = nc.sbuf_base
        wkv_arena = sb("wkv_arena", [P, 3 * KD * D])
        kv_arena = sb("kv_arena", [P, FS * D])
        at_t = nc.sbuf_base
        t_arena = sb("t_arena", [P, KD * B * L])
        at_a = nc.sbuf_base
        a_arena = sb("a_arena", [P, 2 * KD * GL])
        c_arena = sb("c_arena", [P, 2888])
        at_stage = nc.sbuf_base
        stage = sb("stage", [P, KD, D])
        probs_t = sb("probs_t", [P, 800])
        normed = sb("normed", [L, 2, D])
        mask_row = sb("mask_row", [GB, NG * M], mybir.dt.uint8)
        mask_bias = sb("mask_bias", [GB, NG * M], BF16)
        batch_row = sb("batch_row", [GB, GB, L], BF16)
        mask_any = sb("mask_any", [B, HEAD_ROWS], mybir.dt.uint8)
        flag_a = sb("flag_a", [32, 32])
        flag_b = sb("flag_b", [32, 32])
        flag = sb("flag", [1, 4], I32)
        ident = sb("ident", [P, P])
        pick = sb("pick", [P, B])
        ones = sb("ones", [1, B])
        warm = sb("warm", [1, 2])
        minus_half = sb("minus_half", [L, B])
        vecs = sb("vecs", [P, 5, KD])
        pn_vecs = sb("pn_vecs", [P, 2, KD])
        d1b = sb("d1b", [P, KD, FJ])
        half_gate_b = sb("half_gate_b", [P, KD])
        st = sb("st", [L, GB, 6])
        mv = sb("mv", [L, GB, 2])
        vr = sb("vr", [L, GB])
        rstd = sb("rstd", [L, GB])
        st1 = sb("st1", [L, GB, 6])
        mv1 = sb("mv1", [L, GB, 2])
        mean1 = sb("mean1", [L, B])
        vr1 = sb("vr1", [L, B])
        rstd1 = sb("rstd1", [L, B])
        row_max = sb("row_max", [L, 2, 8])
        row_sum = sb("row_sum", [L, 2, 8])
        row_inv = sb("row_inv", [L, 2, 8])
        th_st = sb("th_st", [B, 6])
        th_mv = sb("th_mv", [B, 2])
        th_var = sb("th_var", [B, 1])
        th_rstd = sb("th_rstd", [B, 1])
        o_sum, o_minus, o_squares, o_var, o_rstd = (
            sb(n, [L, GB]) for n in ("o_sum", "o_minus", "o_squares", "o_var", "o_rstd"))

        wk = wkv_arena[:, 0:KD * D].rearrange("p (k n) -> p k n", k=KD)
        agg, bc = (o_arena[:, i * KD * D:(i + 1) * KD * D].rearrange("p (k n) -> p k n", k=KD) for i in range(2))
        wq_h, wq_l, wg_h, wg_l = parts_at([("wq_h", D), ("wq_l", D), ("wg_h", D), ("wg_l", D)], at_w)
        wo_h, wo_l = parts_at([("wo_h", D), ("wo_l", D)], at_o)
        wv_h, wv_l = parts_at([("wv_h", D), ("wv_l", D)], at_kv + KD * D * 4)
        fg_h, fg_l = parts_at([("fg_h", D), ("fg_l", D)], at_kv)
        x_h, x_l = parts_at([("x_h", GL), ("x_l", GL)], at_t + 2 * KD * GL * 4)
        x2a_h, x2a_l = parts_at([("x2a_h", GL), ("x2a_l", GL)], at_w)
        att_h, att_l = parts_at([("att_h", GL), ("att_l", GL)], at_a)
        ctx_h, ctx_l = [None] * 2, [None] * 2
        ctx_h[0], ctx_l[0], ctx_h[1], ctx_l[1] = parts_at(
            [("ctx_h0", P), ("ctx_l0", P), ("ctx_h1", P), ("ctx_l1", P)], at_stage)
        a_raw = a_arena[:, 0:KD * D].rearrange("p (k n) -> p k n", k=KD)
        split = {"wq": (a_raw, wq_h, wq_l, True), "wg": (a_raw, wg_h, wg_l, True),
                 "wv": (stage, wv_h, wv_l, False),
                 "wo": (stage, wo_h, wo_l, False), "fg": (stage, fg_h, fg_l, False)}
        d1 = w_arena[:, :].rearrange("p (k n) -> p k n", k=KD)
        KCOLS = NH * M
        keys = kv_arena[:, 0:KCOLS]
        values = kv_arena[:, KCOLS:KCOLS + GB * D].rearrange("p (c n) -> p c n", c=GB)
        d2 = kv_arena[:, :].rearrange("p (k n) -> p k n", k=FS)
        q_t, gate_t = (t_arena[:, i * KD * GL:(i + 1) * KD * GL].rearrange("p (k n) -> p k n", k=KD)
                       for i in range(2))
        gates = t_arena[:, :].rearrange("p (g k n) -> p g k n", g=NG, k=KD)
        ctx_t = c_arena[:, 0:KD * M]
        UNIT = 722
        probs = [c_arena[0:L, KD * M + i * UNIT:KD * M + (i + 1) * UNIT] for i in range(2)]
        hid = parts = c_arena[:, 0:D]
        z_t = c_arena[:, D:D + FS * B]
        thought = c_arena[0:B, 800:800 + D]
        hid_t = c_arena[:, 800 + D:800 + D + FS * 32].rearrange("p (f n) -> p f n", f=FS)
        rest = 800 + D + FS * 32
        th_t = c_arena[:, rest:rest + KD * 32].rearrange("p (k n) -> p k n", k=KD)
        th_t0, bc_half = (c_arena[:, rest + KD * (32 + i * B):rest + KD * (32 + (i + 1) * B)].rearrange(
            "p (k n) -> p k n", k=KD) for i in range(2))
        last_row, th_norm = stage[0:B, 0, :], stage[0:B, 1, :]
        agg_b, d2_b = stage[0:1, 2, :], stage[0:1, 3, :]
        gamma_row, beta_row = (w_arena[0:L, i * D:(i + 1) * D] for i in range(2))
        lift = c_arena[:, 0:GB * KD * L].rearrange("p (s k n) -> p s k n", s=GB, k=KD)
        mixed = kv_arena[0:L, 0:GB * D].rearrange("p (s n) -> p s n", s=GB)
        final = kv_arena[0:L, GB * D:2 * GB * D].rearrange("p (s n) -> p s n", s=GB)
        squares = kv_arena[0:L, 2 * GB * D:3 * GB * D].rearrange("p (s n) -> p s n", s=GB)
        norm_w, in_gamma, in_beta, gate_b, bc_b = (vecs[:, i, :] for i in range(5))
        pn_gamma, pn_beta = (pn_vecs[:, i, :] for i in range(2))

        ps_s = ctx.enter_context(nc.psum_tensor("ps_s", [P, 2, 512], F32))
        ps_pt = ctx.enter_context(nc.psum_tensor("ps_pt", [P, 2, 512], F32))
        ps_mm = [ctx.enter_context(nc.psum_tensor(f"ps_mm{i}", [P, 512], F32)) for i in range(2)]
        ps_pv = ctx.enter_context(nc.psum_tensor("ps_pv", [P, 512], F32))
        ps_tr = ctx.enter_context(nc.psum_tensor("ps_tr", [P, 512], F32))

        back_bank = [ps_mm[0], ps_mm[1], ps_tr, ps_pt[:, 0, :]]

        x_first_loaded, x_rest_loaded, ctx_loaded, const_loaded, mask_loaded, mask_row_loaded, row_loaded = (
            sem(n) for n in ("x_first_loaded", "x_rest_loaded", "ctx_loaded", "const_loaded", "mask_loaded",
                             "mask_row_loaded", "row_loaded"))
        w_loaded = {n: sem(f"{n}_loaded") for n in ("wq", "wk", "wg", "wv", "wo", "fg", "agg", "bc", "d1", "d2")}
        last_row_loaded, bias_row_loaded, out_row_loaded = (
            sem(n) for n in ("last_row_loaded", "bias_row_loaded", "out_row_loaded"))
        stored = [sem(f"stored{s}") for s in range(GB)]
        warmed = sem("warmed")
        filled, zeroed, hid_zeroed, bias_made, picks_made, flag_step, flag_set, half_made = (
            sem(n) for n in ("filled", "zeroed", "hid_zeroed", "bias_made", "picks_made", "flag_step", "flag_set",
                             "half_made"))
        high_made = {n: sem(f"{n}_high_made") for n in ("wq", "wg", "wv", "wo", "fg")}
        low_made = {n: sem(f"{n}_low_made") for n in ("wq", "wg", "wv", "wo", "fg")}
        ctx_high_made, ctx_low_made = sem("ctx_high_made"), sem("ctx_low_made")
        st_made, mv_made, var_ready, rstd_ready, norm_ready = (
            sem(n) for n in ("st_made", "mv_made", "var_ready", "rstd_ready", "norm_ready"))
        xt_done, xt_high, xt_kept, back1_done = (sem(n) for n in ("xt_done", "xt_high", "xt_kept", "back1_done"))
        done = {k: sem(f"{k}_done") for k in ("q", "k", "v", "g", "o", "fg")}
        kept = {k: sem(f"{k}_kept") for k in ("q", "k", "v", "g", "o", "fg")}
        (scored, maxed, shifted, raised, summed, inverted, weighted, divided, turned, turn_kept, mixed_v,
         mix_high, mix_kept) = (sem(n) for n in (
             "scored", "maxed", "shifted", "raised", "summed", "inverted", "weighted", "divided",
             "turned", "turn_kept", "mixed_v", "mix_high", "mix_kept"))
        x1_ready, st1_made, mv1_made, mean1_ready, var1_ready, rstd1_ready = (
            sem(n) for n in ("x1_ready", "st1_made", "mv1_made", "mean1_ready", "var1_ready", "rstd1_ready"))
        norm2_ready, tr2_done, tr2_high, tr2_used = (
            sem(n) for n in ("norm2_ready", "tr2_done", "tr2_high", "tr2_used"))
        th_ready, th_st_made, th_mv_made, th_var_ready, th_rstd_ready, th_normed = (
            sem(n) for n in ("th_ready", "th_st_made", "th_mv_made", "th_var_ready", "th_rstd_ready", "th_normed"))
        th_kept = sem("th_kept")
        (tht_done, tht_scaled, tht_ready, up_done, up_kept, upt_done, z_ready, hid_ready, down_done,
         down_kept) = (sem(n) for n in (
             "tht_done", "tht_scaled", "tht_ready", "up_done", "up_kept", "upt_done", "z_ready",
             "hid_ready", "down_done", "down_kept"))
        bc_done, bc_ready = sem("bc_done"), sem("bc_ready")
        (lifted, back_done, o_ready, o_minus_ready, o_squares_ready, o_var_ready, o_rstd_ready,
         o_scaled, x_biased, out_ready) = (sem(n) for n in (
             "lifted", "back_done", "o_ready", "o_minus_ready", "o_squares_ready", "o_var_ready",
             "o_rstd_ready", "o_scaled", "x_biased", "out_ready"))

        tail, full = Geometry(False), Geometry(True)

        def first_splits(u):
            return {0: [("wg", 0), ("wg", 1)], 1: [("wg", 2), ("wg", 3)],
                    5: [("wo", 0)], 6: [("wo", 1), ("wo", 2)], 7: [("wo", 3)]}.get(u, [])

        def fg_splits(u):
            return {5: [0], 6: [1, 2], 7: [3]}.get(u, [])

        def ctx_tile(geo, c):
            first, rows = geo.chunks[c] if geo.full else (c * TAIL, TAIL)
            raw = ctx_t[:, 0:KD * geo.lot_keys].rearrange("p (k n) -> p k n", k=KD)
            return raw[:, :, first:first + rows], rows

        def x2_parts(s):
            return ((x2a_h, x2a_l), (x_h, x_l))[s] if isinstance(s, int) else (att_h, att_l)

        def x2_bank(s, b):
            return ps_tr if isinstance(s, int) or b % 2 == 0 else ps_mm[1]

        def gates_of(g, s):
            return gates[:, bass.ds(g, 1), :, s * L:(s + 1) * L].rearrange("p a k n -> p (a k) n")

        def mixed_view(geo, u, b, att):
            if geo.full:
                r = slice(64 * (u % 2), 64 * (u % 2) + 64)
                return att[r, u // 2, b * L:(b + 1) * L], ps_pv[r, 0:L]
            t = 2 * (u % 2)
            return att[:, t:t + 2, b * L:(b + 1) * L], ps_pv[:, 0:2 * L].rearrange("p (k n) -> p k n", k=2)

        def each_group(eng, body):
            body(0, False)
            with eng.Fori(1, NG - 1) as g:
                body(g, False)
            body(NG - 1, True)

        def is_first(g):
            return isinstance(g, int) and g == 0

        def each_out(eng, body):
            for s in range(GB):
                body(0, s)
            with eng.Fori(1, NG - 1) as g:
                for s in range(GB):
                    body(g, s)
            for s in range(GB):
                body(NG - 1, s)

        passed = {n: sem(f"{n}_passed") for n in ("pe", "act", "dve", "pool")}

        def wait_apart(name, eng, signal, value):
            eng.wait_ge(signal, value)
            eng.sem_inc(passed[name], 1)

        def branch(eng, tail_part, full_part):
            eng.wait_ge(flag_set, 1)
            seen = eng.value_load(flag[0:1, 0:1], min_val=0, max_val=1)
            with eng.If(seen > 0):
                full_part()
            with eng.Else():
                tail_part()

        block = ctx.enter_context(nc.Block())

        @block.sync
        def _(sp):
            def load_x(first, n, signal):
                sp.dma_start(x[:, first:first + n, :],
                             a["x"][first:first + n].rearrange("b l d -> l b d")).then_inc(signal, 16)

            def load_w(name, dst):
                sp.dma_start(dst, a[name]).then_inc(w_loaded[name], 16)

            def load_ctx(geo, i):
                src = a["ctx_full"] if geo.full else a["ctx_tail"]
                sp.dma_start(ctx_t[:, 0:KD * geo.lot_keys],
                             src[bass.ds(i, 1)].rearrange("a p n -> p (a n)")).then_inc(ctx_loaded, 16)

            def load_mask_row(geo):
                src = a["mask_row_full"] if geo.full else a["mask_row_tail"]
                sp.dma_start(mask_row[:, 0:NG * geo.keys], src).then_inc(mask_row_loaded, 16)

            def load_rest(geo):
                load_w("wv", stage[:, :, :])
                load_x(GB, B - GB, x_rest_loaded)
                sp.wait_ge(low_made["wq"], KD)
                load_w("wg", a_raw)
                for dst, name in ((pick, "pick"), (pn_vecs, "pn_vecs"), (d1b, "d1b")):
                    sp.dma_start(dst[:], a[name]).then_inc(row_loaded, 16)
                sp.wait_ge(low_made["wv"], KD)
                if not geo.full:
                    sp.wait_ge(done["v"], geo.v_tiles)
                load_w("wo", stage[:, :, :])

            sp.dma_start(mask_any[:, :], a["mask"][:, 0:HEAD_ROWS]).then_inc(mask_loaded, 16)
            load_w("wk", wk)

            def attend(geo):
                load_ctx(geo, 0)
                load_x(0, GB, x_first_loaded)
                sp.dma_start(ident[:, :], a["ident"]).then_inc(const_loaded, 16)
                sp.dma_start(vecs[:, :, :], a["vecs"]).then_inc(const_loaded, 16)
                load_w("wq", a_raw)
                load_mask_row(geo)
                load_rest(geo)
                with sp.Fori(1, NG * geo.lots) as i:
                    sp.wait_ge(done["v"], geo.v_tiles * i)
                    load_ctx(geo, i)
                sp.wait_ge(low_made["wo"], KD)
                sp.wait_ge(done["v"], geo.v_tiles * NG * geo.lots)
                load_w("fg", stage[:, :, :])

            branch(sp, lambda: attend(tail), lambda: attend(full))
            sp.wait_ge(done["g"], KD * NG)
            sp.wait_ge(done["fg"], KD)
            load_w("d1", d1)
            sp.wait_ge(low_made["fg"], KD)
            for dst, name in ((agg_b, "agg_b"), (d2_b, "d2_b")):
                sp.dma_start(dst, a[name]).then_inc(bias_row_loaded, 16)
            sp.wait_ge(x1_ready, B)
            sp.dma_start(last_row, x[L - 1:L, :, :]).then_inc(last_row_loaded, 16)
            load_w("agg", agg)
            load_w("d2", d2)
            load_w("bc", bc)
            sp.wait_ge(up_done, STEPS)
            for dst, name in ((gamma_row, "out_gamma"), (beta_row, "out_beta")):
                sp.dma_start(dst, a[name].to_broadcast([L, D])).then_inc(out_row_loaded, 16)
            with sp.Fori(0, NG) as g:
                for s in range(GB):
                    sp.wait_ge(out_ready, GB * g + s + 1)
                    sp.dma_start(a["out"][bass.ds(GB * g + s, 1)].rearrange("b l d -> l (b d)"),
                                 final[:, s, :]).then_inc(stored[s], 16)
            for s in range(GB):
                sp.wait_ge(stored[s], 16 * NG)

        @block.tensor
        def _(pe):
            mm_uses = []

            def in_parts(w_high, w_low, t_high, t_low, m):
                cols = slice(m * P, (m + 1) * P)
                return [(w[:, k, cols], t[:, k, :]) for k in range(KD)
                        for w, t in ((w_high, t_high), (w_high, t_low), (w_low, t_high))]

            def project(kind, count, rows, cols, mats, need=()):
                use = len(mm_uses)
                bank = ps_mm[use % 2]
                if use >= 2:
                    kind2, count2 = mm_uses[use - 2]
                    pe.wait_ge(kept[kind2], count2)
                for s, v in need:
                    pe.wait_ge(s, v)
                for n, (lhs, rhs) in enumerate(mats):
                    mm = pe.matmul(bank[0:rows, 0:cols], lhs, rhs, start=(n == 0), stop=(n == len(mats) - 1))
                mm.then_inc(done[kind], 1)
                mm_uses.append((kind, count))

            def turn_x(n, b, after=None):
                if b:
                    pe.wait_ge(xt_kept, GB * n + b)
                elif after is not None:
                    pe.wait_ge(x1_ready, GB * after + GB)
                pe.wait_ge(norm_ready, GB * n + b + 1)
                if is_first(n) and b == 0:
                    pe.wait_ge(const_loaded, 32)
                for k in range(KD):
                    t = pe.transpose(ps_tr[:, k * L:(k + 1) * L], normed[:, b % 2, k * P:(k + 1) * P],
                                     ident[0:L, 0:L])
                t.then_inc(xt_done, 1)

            def project_q(n, m):
                project("q", KD * n + m + 1, P, GL, in_parts(wq_h, wq_l, x_h, x_l, m),
                        [(low_made["wq"], KD), (xt_kept, GB * n + GB)])

            def project_g(n, m):
                project("g", KD * n + m + 1, P, GL, in_parts(wg_h, wg_l, x_h, x_l, m),
                        [(low_made["wg"], KD), (xt_kept, GB * n + GB)])

            def ctx_cols(geo, k):
                return ctx_t[:, k * geo.lot_keys:(k + 1) * geo.lot_keys]

            def project_k(geo, i, m):
                project("k", KD * i + m + 1, P, geo.lot_keys,
                        [(wk[:, k, m * P:(m + 1) * P], ctx_cols(geo, k)) for k in range(KD)],
                        [(w_loaded["wk"], 16), (ctx_loaded, 16 * i + 16)])

            def project_v(geo, i, c):
                _, rows = ctx_tile(geo, c)
                high, low = ctx_h[c % 2][:, :, 0:rows], ctx_l[c % 2][:, :, 0:rows]
                mats = [(t[:, k, :], w[:, k, :]) for k in range(KD)
                        for t, w in ((high, wv_h), (high, wv_l), (low, wv_h))]
                project("v", geo.v_tiles * i + c + 1, rows, D, mats,
                        [(low_made["wv"], KD), (ctx_low_made, geo.v_tiles * i + c + 1)])

            def project_o(g, m):
                project("o", KD * g + m + 1, P, GL, in_parts(wo_h, wo_l, att_h, att_l, m),
                        [(low_made["wo"], KD)])

            def scores(geo, g, lot, u):
                unit = geo.group_units * g + geo.units * lot + u
                i = geo.lots * g + lot
                b = geo.batch(lot, u)
                if u == 0 and not geo.full:
                    pe.wait_ge(kept["q"], KD * g + KD // 2)
                elif u < 2:
                    pe.wait_ge(kept["q"], KD * g + KD)
                if u == 0:
                    pe.wait_ge(kept["k"], KD * i + KD)
                if u or lot:
                    pe.wait_ge(shifted, unit)
                w = geo.bank_heads * geo.keys
                for k in range(2):
                    h0 = geo.heads(u, k)[0]
                    col = (h0 if geo.full else NH * b + h0) * geo.keys
                    bank = ps_s[0:L, k, 0:w]
                    pe.matmul(bank, q_t[:, h0 // 4, b * L:(b + 1) * L], keys[:, col:col + w], start=True, stop=False)
                    bias = mask_bias[:, bass.ds(g * geo.keys, geo.keys)]
                    if geo.bank_heads > 1:
                        bias = bias.unsqueeze(1).to_broadcast([GB, geo.bank_heads, geo.keys])
                    mm = pe.matmul(bank, batch_row[:, b, :], bias, start=False, stop=True)
                mm.then_inc(scored, 1)

            def turn_probs(geo, g, lot, u):
                unit = geo.group_units * g + geo.units * lot + u
                if u or lot:
                    pe.wait_ge(turn_kept, unit)
                pe.wait_ge(divided, unit + 1)
                for k in range(2):
                    n = 0
                    for j, _ in enumerate(geo.heads(u, k)):
                        for first, rows in geo.chunks:
                            col = (k * geo.bank_heads + j) * geo.keys + first
                            t = pe.transpose(ps_pt[0:rows, k, n * L:(n + 1) * L], probs[u % 2][:, col:col + rows],
                                             ident[0:L, 0:L])
                            n += 1
                t.then_inc(turned, 1)

            def mix_values(geo, g, lot, u):
                unit = geo.group_units * g + geo.units * lot + u
                pe.wait_ge(turn_kept, unit + 1)
                if u or lot:
                    pe.wait_ge(mix_kept, unit)
                i = geo.lots * g + lot
                pe.wait_ge(kept["v"], geo.v_tiles * i + (geo.v_tiles if geo.full else geo.batch(lot, u) + 1))
                n = 0
                for k in range(2):
                    for h in geo.heads(u, k):
                        r = HD * (h % 4)
                        out = ps_pv[r:r + HD, (0 if geo.full else k) * L:((0 if geo.full else k) + 1) * L]
                        for c, (first, rows) in enumerate(geo.chunks):
                            v = values[0:rows, c if geo.full else geo.batch(lot, u), h * HD:(h + 1) * HD]
                            mm = pe.matmul(out, v, probs_t[0:rows, n * L:(n + 1) * L], start=(c == 0),
                                           stop=(c == len(geo.chunks) - 1))
                            n += 1
                mm.then_inc(mixed_v, 1)

            def turn_back(g, b, bank=ps_tr):
                if b and bank is ps_tr:
                    pe.wait_ge(x1_ready, GB * g + b)
                pe.wait_ge(kept["o"], KD * g + KD)
                for k in range(KD):
                    t = pe.transpose(bank[0:L, k * P:(k + 1) * P], gate_t[:, k, b * L:(b + 1) * L], ident[:, :])
                t.then_inc(back1_done, 1)

            def turn_x2(s, b):
                if isinstance(s, int):
                    if s or b:
                        pe.wait_ge(tr2_used, GB * s + b)
                elif b == 1:
                    pe.wait_ge(kept["fg"], KD * s)
                elif b >= 2:
                    pe.wait_ge(tr2_used, GB * s + b - 1)
                pe.wait_ge(norm2_ready, GB * s + b + 1)
                for k in range(KD):
                    t = pe.transpose(x2_bank(s, b)[:, k * L:(k + 1) * L], normed[:, b % 2, k * P:(k + 1) * P],
                                     ident[0:L, 0:L])
                t.then_inc(tr2_done, 1)

            def gate(s, m):
                project("fg", KD * s + m + 1, P, GL, in_parts(fg_h, fg_l, *x2_parts(s), m),
                        [(low_made["fg"], KD), (tr2_used, GB * s + GB)])

            def tail_part():
                mm_uses[:] = []
                project_k(tail, 0, 0)
                for b in range(GB - 1):
                    project_k(tail, 0, b + 1)
                    turn_x(0, b)
                turn_x(0, GB - 1)
                for m in range(KD):
                    project_q(0, m)

                def body(g, last):
                    mm_uses[:] = [("q", KD - 1), ("q", KD)] if is_first(g) else [("o", KD * g - 1), ("o", KD * g)]
                    for u in range(tail.units):
                        scores(tail, g, 0, u)
                        if u >= 2:
                            turn_probs(tail, g, 0, u - 2)
                        if u < GB:
                            project_v(tail, g, u)
                            if not is_first(g):
                                turn_back(g - 1, u)
                        else:
                            project_g(g, u - GB)
                        if u >= 2:
                            mix_values(tail, g, 0, u - 2)
                        if last and u >= GB:
                            if u == GB:
                                pe.wait_ge(x1_ready, GB * g)
                            turn_x2(0, u - GB)
                    n = g + 1
                    if not last:
                        turn_x(n, 0, None if is_first(g) else g - 1)
                        project_k(tail, n, 0)
                        turn_x(n, 1)
                        turn_probs(tail, g, 0, 6)
                        project_k(tail, n, 1)
                        mix_values(tail, g, 0, 6)
                        turn_x(n, 2)
                        project_k(tail, n, 2)
                        turn_x(n, 3)
                        turn_probs(tail, g, 0, 7)
                        project_k(tail, n, 3)
                        mix_values(tail, g, 0, 7)
                        for m in range(KD):
                            project_q(n, m)
                    else:
                        gate(0, 0)
                        turn_x2(1, 0)
                        turn_probs(tail, g, 0, 6)
                        mix_values(tail, g, 0, 6)
                        gate(0, 1)
                        turn_x2(1, 1)
                        turn_probs(tail, g, 0, 7)
                        gate(0, 2)
                        turn_x2(1, 2)
                        mix_values(tail, g, 0, 7)
                        gate(0, 3)
                        turn_x2(1, 3)
                    pe.wait_ge(mix_kept, tail.units * g + tail.units)
                    for m in range(KD):
                        project_o(g, m)
                    if last:
                        for b, bank in enumerate((ps_tr, ps_pt[:, 0, :], ps_pt[:, 1, :], ps_s[:, 0, :])):
                            turn_back(g, b, bank)

                pe.wait_ge(bias_made, 1)
                pe.wait_ge(picks_made, 1)
                each_group(pe, body)

            def full_part():
                pe.wait_ge(bias_made, 1)
                pe.wait_ge(picks_made, 1)
                with pe.Fori(0, NG) as g:
                    mm_uses[:] = []
                    for b in range(GB):
                        turn_x(g, b)
                    for m in range(KD):
                        project_q(g, m)
                    for m in range(KD):
                        project_g(g, m)
                    for lot in range(GB):
                        for m in range(KD):
                            project_k(full, GB * g + lot, m)
                        for c in range(full.v_tiles):
                            project_v(full, GB * g + lot, c)
                        for u in range(full.units):
                            scores(full, g, lot, u)
                            if u >= 2:
                                turn_probs(full, g, lot, u - 2)
                                mix_values(full, g, lot, u - 2)
                        for u in (6, 7):
                            turn_probs(full, g, lot, u)
                            mix_values(full, g, lot, u)
                    pe.wait_ge(mix_kept, full.group_units * g + full.group_units)
                    for m in range(KD):
                        project_o(g, m)
                    for b in range(GB):
                        turn_back(g, b)
                    pe.wait_ge(x1_ready, GB * g + GB)
                mm_uses[:] = [("o", KD * NG - 1), ("o", KD * NG)]
                for s in range(2):
                    for b in range(GB):
                        turn_x2(s, b)
                for m in range(KD):
                    gate(0, m)

            branch(pe, tail_part, full_part)
            pe.wait_ge(filled, 2)

            parts_of_gate = 3 * KD

            def gate_products(n, first, count):
                for i in range(first, first + count):
                    m, j = divmod(i, parts_of_gate)
                    if j == 0:
                        pe.wait_ge(kept["fg"], KD * n + m - 1)
                        pe.wait_ge(tr2_used, GB * n + GB)
                    lhs, rhs = in_parts(fg_h, fg_l, *x2_parts(n), m)[j]
                    mm = pe.matmul(ps_mm[m % 2][:, 0:GL], lhs, rhs, start=(j == 0), stop=(j == parts_of_gate - 1))
                    if j == parts_of_gate - 1:
                        mm.then_inc(done["fg"], 1)

            def turn_thought(i):
                wait_apart("pe", pe, th_normed, i + 1)
                for k in range(KD):
                    t = pe.transpose(ps_pt[:, 1, k * B:(k + 1) * B], th_norm[:, k * P:(k + 1) * P], ident[0:B, 0:B])
                t.then_inc(tht_done, 1)

            def think(s, n, half):
                turn_thought(s + 1)
                if half == 0:
                    turn_x2(n, 0)
                else:
                    gate_products(n, 20, 4)
                pe.wait_ge(tht_ready, s + 2)
                for k in range(KD):
                    for j in range(FJ):
                        mm = pe.matmul(ps_s[32 * j:32 * j + 32, 0, :], th_t[:, k, :], d1[:, k, j * D:(j + 1) * D],
                                       start=(k == 0), stop=(k == KD - 1))
                mm.then_inc(up_done, 1)
                if half == 0:
                    turn_x2(n, 1)
                else:
                    gate_products(n, 24, 4)
                pe.wait_ge(up_kept, s + 1)
                for i in range(KD):
                    t = pe.transpose(ps_pt[:, 0, i * P:(i + 1) * P], hid[:, i * P:(i + 1) * P], ident[:, :])
                t.then_inc(upt_done, 1)
                if half == 0:
                    turn_x2(n, 2)
                else:
                    gate_products(n, 28, 6)
                pe.wait_ge(w_loaded["d2"], 16)
                pe.wait_ge(hid_ready, s + 1)
                for i in range(KD):
                    for j in range(FJ):
                        mm = pe.matmul(ps_s[32 * j:32 * j + 32, 1, :], hid_t[:, KD * i + j, :], d2[:, KD * j + i, :],
                                       start=(i == 0), stop=(i == KD - 1))
                mm.then_inc(down_done, 1)
                if half == 0:
                    turn_x2(n, 3)
                pe.matmul(ps_pv[0:B, :], ones[:, :], d2_b, start=True, stop=False)
                wait_apart("pe", pe, th_kept, s + 1)
                pe.matmul(ps_pv[0:B, :], ident[0:B, 0:B], thought, start=False, stop=False)
                pe.wait_ge(down_kept, s + 1)
                pe.matmul(ps_pv[0:B, :], pick[:, :], parts, start=False, stop=True).then_inc(th_ready, 1)
                if half == 0:
                    gate_products(n, 0, 20)
                else:
                    gate_products(n, 34, 14)

            mm_uses[:] = [("fg", KD - 1), ("fg", KD)]
            pe.wait_ge(kept["o"], KD * NG)
            for m in range(KD - 1):
                gate(1, m)
            turn_thought(0)
            pe.wait_ge(w_loaded["agg"], 16)
            pe.wait_ge(row_loaded, 16 * 3)
            pe.wait_ge(bias_row_loaded, 32)
            pe.wait_ge(tht_ready, 1)
            for k in range(KD):
                pe.matmul(ps_pv[0:B, :], th_t[:, k, 0:B], agg[:, k, :], start=(k == 0), stop=False)
            pe.matmul(ps_pv[0:B, :], ones[:, :], agg_b, start=False, stop=True).then_inc(th_ready, 1)
            gate(1, KD - 1)
            pe.wait_ge(w_loaded["d1"], 16)
            pe.wait_ge(hid_zeroed, 2)
            with pe.Fori(0, STEPS // 2) as i:
                for half in range(2):
                    think(2 * i + half, i + 2, half)
            pe.wait_ge(th_kept, STEPS + 1)
            for k in range(KD):
                t = pe.transpose(ps_pt[:, 1, k * B:(k + 1) * B], thought[:, k * P:(k + 1) * P], ident[0:B, 0:B])
            t.then_inc(tht_done, 1)
            pe.wait_ge(w_loaded["bc"], 16)
            pe.wait_ge(tht_ready, STEPS + 2)
            for k in range(KD):
                mm = pe.matmul(ps_s[32 * k:32 * k + 32, 0, :], th_t[:, k, :], bc[:, k, :], start=True, stop=True)
            mm.then_inc(up_done, 1)
            pe.wait_ge(up_kept, STEPS + 1)
            for m in range(KD):
                mm = pe.matmul(ps_pv[:, m * B:(m + 1) * B], hid[:, m * P:(m + 1) * P], pick[:, :], start=True,
                               stop=True)
            mm.then_inc(bc_done, 1)

            def back(g, s):
                i = GB * g + s
                pe.wait_ge(lifted, i + 1)
                if not is_first(g):
                    pe.wait_ge(o_ready, i - GB + 1)
                for k in range(KD):
                    t = pe.transpose(back_bank[s][0:L, k * P:(k + 1) * P], lift[:, s, k, :], ident[:, :])
                t.then_inc(back_done, 1)

            each_out(pe, back)

        @block.scalar
        def _(act):
            act.wait_ge(filled, 2)
            act.activation(warm[:, 0:1], ones[:, 0:1], ACT.Exp).then_inc(warmed, 1)

            def split_high(name, k, values_made=None):
                raw, high, _, scaled = split[name]
                act.wait_ge(w_loaded[name], 16)
                if scaled:
                    act.wait_ge(const_loaded, 32)
                    c = act.activation(high[:, k, :], raw[:, k, :], ACT.Copy, scale=norm_w[:, k:k + 1])
                else:
                    if values_made:
                        act.wait_ge(done["v"], values_made)
                    c = act.activation(high[:, k, :], raw[:, k, :], ACT.Copy)
                c.then_inc(high_made[name], 1)

            def keep_x_high(n, b):
                act.wait_ge(xt_done, GB * n + b + 1)
                act.activation(x_h[:, :, b * L:(b + 1) * L], ps_tr[:, 0:GL].rearrange("p (k n) -> p k n", k=KD),
                               ACT.Copy).then_inc(xt_high, 1)

            def keep_x2(s, b):
                act.wait_ge(tr2_done, GB * s + b + 1)
                act.activation(x2_parts(s)[0][:, :, b * L:(b + 1) * L],
                               x2_bank(s, b)[:, 0:GL].rearrange("p (k n) -> p k n", k=KD), ACT.Copy
                               ).then_inc(tr2_high, 1)

            def keep_gate(s, m):
                if isinstance(s, int) and s == 0 and m == 0:
                    act.wait_ge(half_made, 1)
                act.wait_ge(done["fg"], KD * s + m + 1)
                act.activation(gates[:, bass.ds(s, 1), m, :].rearrange("p a n -> p (a n)"), ps_mm[m % 2][:, 0:GL],
                               ACT.Tanh, bias=half_gate_b[:, m:m + 1], scale=0.5).then_inc(kept["fg"], 1)

            def keep_q(n, m):
                act.wait_ge(done["q"], KD * n + m + 1)
                act.activation(q_t[:, m, :], ps_mm[m % 2][:, 0:GL], ACT.Copy).then_inc(kept["q"], 1)

            def keep_g(n, m):
                act.wait_ge(done["g"], KD * n + m + 1)
                act.activation(gate_t[:, m, :], ps_mm[m % 2][:, 0:GL], ACT.Tanh, scale=0.5).then_inc(kept["g"], 1)

            def keep_k(geo, i, m, bank):
                act.wait_ge(done["k"], KD * i + m + 1)
                for j in range(4):
                    r = slice(HD * j, HD * j + HD)
                    if geo.full:
                        dst = keys[r, (4 * m + j) * M:(4 * m + j + 1) * M]
                        src = bank[r, 0:M]
                    else:
                        dst = keys[r, 0:GB * NH * TAIL].rearrange("p (b h n) -> p b h n", b=GB, h=NH)[:, :, 4 * m + j, :]
                        src = bank[r, 0:GB * TAIL].rearrange("p (b n) -> p b n", b=GB)
                    c = act.activation(dst, src, ACT.Copy)
                c.then_inc(kept["k"], 1)

            def keep_v(geo, i, c, bank):
                rows = geo.chunks[c][1] if geo.full else TAIL
                act.wait_ge(done["v"], geo.v_tiles * i + c + 1)
                act.activation(values[0:rows, c, :], bank[0:rows, :], ACT.Copy).then_inc(kept["v"], 1)

            def split_ctx_high(geo, i, c):
                if c < 2:
                    act.wait_ge(done["k"], KD * i + KD)
                    act.wait_ge(low_made["wv" if is_first(i) else "wo"], KD)
                else:
                    act.wait_ge(done["v"], geo.v_tiles * i + c - 1)
                raw, rows = ctx_tile(geo, c)
                act.activation(ctx_h[c % 2][:, :, 0:rows], raw, ACT.Copy).then_inc(ctx_high_made, 1)

            def raise_(geo, g, lot, u):
                unit = geo.group_units * g + geo.units * lot + u
                act.wait_ge(shifted, unit + 1)
                w = geo.unit_heads * geo.keys
                act.activation(probs[u % 2][:, 0:w], probs[u % 2][:, 0:w], ACT.Exp, scale=SCALE).then_inc(raised, 1)

            def keep_turned(geo, g, lot, u):
                unit = geo.group_units * g + geo.units * lot + u
                act.wait_ge(turned, unit + 1)
                if geo.full:
                    whole = [c for c in geo.chunks if c[1] == P]
                    w, rest = len(whole) * L, geo.chunks[-1][1]
                    dst = probs_t[:, 0:6 * L].rearrange("p (k n) -> p k n", k=2)
                    act.activation(dst[:, :, 0:w], ps_pt[:, :, 0:w], ACT.Copy)
                    act.activation(dst[0:rest, :, w:w + L], ps_pt[0:rest, :, w:w + L], ACT.Copy).then_inc(turn_kept, 1)
                else:
                    dst = probs_t[0:TAIL, :].rearrange("p (k n) -> p k n", k=2)
                    act.activation(dst, ps_pt[0:TAIL, :, 0:4 * L], ACT.Copy).then_inc(turn_kept, 1)

            def keep_mixed(geo, g, lot, u):
                unit = geo.group_units * g + geo.units * lot + u
                b = geo.batch(lot, u)
                act.wait_ge(mixed_v, unit + 1)
                dst, src = mixed_view(geo, u, b, att_h)
                act.activation(dst, src, ACT.Copy).then_inc(mix_high, 1)

            def tail_part():
                act.wait_ge(zeroed, 1)
                keep_k(tail, 0, 0, ps_mm[0])
                for b in range(GB - 1):
                    keep_k(tail, 0, b + 1, ps_mm[(b + 1) % 2])
                    keep_x_high(0, b)
                keep_x_high(0, GB - 1)
                for k in range(KD):
                    split_high("wv", k)
                for m in range(KD):
                    keep_q(0, m)
                    if m < 2:
                        split_ctx_high(tail, 0, m)

                def body(g, last):
                    for u in range(tail.units):
                        if u >= 2:
                            keep_turned(tail, g, 0, u - 2)
                        raise_(tail, g, 0, u)
                        if u < GB:
                            keep_v(tail, g, u, ps_mm[u % 2])
                            if u + 2 < GB:
                                split_ctx_high(tail, g, u + 2)
                        else:
                            keep_g(g, u - GB)
                        if u == 2 and is_first(g):
                            act.wait_ge(low_made["wg"], KD)
                        if u >= 2:
                            keep_mixed(tail, g, 0, u - 2)
                        if is_first(g):
                            for name, k in first_splits(u):
                                split_high(name, k)
                        if last and u >= GB:
                            keep_x2(0, u - GB)
                            for k in fg_splits(u):
                                split_high("fg", k, tail.v_tiles * NG)
                    n = g + 1
                    if last:
                        keep_gate(0, 0)
                        keep_x2(1, 0)
                        keep_turned(tail, g, 0, 6)
                        keep_mixed(tail, g, 0, 6)
                        keep_gate(0, 1)
                        keep_x2(1, 1)
                        keep_turned(tail, g, 0, 7)
                        keep_gate(0, 2)
                        keep_x2(1, 2)
                        keep_mixed(tail, g, 0, 7)
                        keep_gate(0, 3)
                        keep_x2(1, 3)
                        return
                    keep_x_high(n, 0)
                    keep_k(tail, n, 0, ps_mm[0])
                    keep_x_high(n, 1)
                    keep_turned(tail, g, 0, 6)
                    keep_k(tail, n, 1, ps_mm[1])
                    keep_mixed(tail, g, 0, 6)
                    keep_x_high(n, 2)
                    keep_k(tail, n, 2, ps_mm[0])
                    keep_x_high(n, 3)
                    keep_turned(tail, g, 0, 7)
                    keep_k(tail, n, 3, ps_mm[1])
                    keep_mixed(tail, g, 0, 7)
                    for c in range(2):
                        split_ctx_high(tail, n, c)
                    for m in range(KD):
                        keep_q(n, m)

                each_group(act, body)

            def full_part():
                for name in ("wv", "wg", "wo"):
                    for k in range(KD):
                        split_high(name, k)
                act.wait_ge(low_made["wg"], KD)
                act.wait_ge(zeroed, 1)
                with act.Fori(0, NG) as g:
                    for b in range(GB):
                        keep_x_high(g, b)
                    for m in range(KD):
                        keep_q(g, m)
                    for m in range(KD):
                        keep_g(g, m)
                    uses = 2 * KD
                    for lot in range(GB):
                        for m in range(KD):
                            keep_k(full, GB * g + lot, m, ps_mm[(uses + m) % 2])
                        uses += KD
                        i = GB * g + lot
                        split_ctx_high(full, i, 0)
                        split_ctx_high(full, i, 1)
                        for c in range(full.v_tiles):
                            keep_v(full, i, c, ps_mm[(uses + c) % 2])
                            if c + 2 < full.v_tiles:
                                split_ctx_high(full, i, c + 2)
                        uses += full.v_tiles
                        for u in range(full.units):
                            raise_(full, g, lot, u)
                            if u >= 2:
                                keep_turned(full, g, lot, u - 2)
                                keep_mixed(full, g, lot, u - 2)
                        for u in (6, 7):
                            keep_turned(full, g, lot, u)
                            keep_mixed(full, g, lot, u)
                for k in range(KD):
                    split_high("fg", k, full.v_tiles * NG * GB)
                for s in range(2):
                    for b in range(GB):
                        keep_x2(s, b)
                for m in range(KD):
                    keep_gate(0, m)

            branch(act, tail_part, full_part)

            for m in range(KD - 1):
                keep_gate(1, m)

            keep_gate(1, KD - 1)

            def think(s, n, half):
                act.activation(warm[:, 1:2], ones[:, 0:1], ACT.Gelu).then_inc(warmed, 1)
                if half == 0:
                    keep_x2(n, 0)
                else:
                    keep_gate(n, 1)
                act.wait_ge(up_done, s + 1)
                act.activation(hid, ps_s[:, 0, :], ACT.Copy).then_inc(up_kept, 1)
                if half == 0:
                    keep_x2(n, 1)
                act.wait_ge(z_ready, s + 1)
                act.activation(hid_t[:, :, 0:B], z_t.rearrange("p (f b) -> p f b", f=FS),
                               ACT.Gelu).then_inc(hid_ready, 1)
                if half == 0:
                    keep_x2(n, 2)
                act.wait_ge(down_done, s + 1)
                act.activation(parts, ps_s[:, 1, :], ACT.Copy).then_inc(down_kept, 1)
                if half == 0:
                    keep_x2(n, 3)
                    keep_gate(n, 0)
                else:
                    keep_gate(n, 2)
                    keep_gate(n, 3)

            with act.Fori(0, STEPS // 2) as i:
                for half in range(2):
                    think(2 * i + half, i + 2, half)

            act.wait_ge(up_done, STEPS + 1)
            act.activation(hid, ps_s[:, 0, :], ACT.Copy).then_inc(up_kept, 1)

            def raise_gate(g, s):
                i = GB * g + s
                if not is_first(g):
                    act.wait_ge(back_done, i - GB + 1)
                for k in range(KD):
                    row = bc_half[:, k, bass.ds(i, 1)]
                    c = act.activation(lift[:, s, k, :], gates_of(g, s)[:, k, :], ACT.Identity, bias=row,
                                       scale=row)
                c.then_inc(lifted, 1)

            def measure_out(g, s):
                i = GB * g + s
                if not (isinstance(g, int) and i >= NG * GB - 2):
                    raise_gate(g + (s + 2) // GB, (s + 2) % GB)
                act.wait_ge(o_minus_ready, i + 1)
                act.activation(squares[:, s, :], mixed[:, s, :], ACT.Square, bias=o_minus[:, s:s + 1],
                               accum_out=o_squares[:, s:s + 1]).then_inc(o_squares_ready, 1)

            act.wait_ge(bc_ready, KD)
            raise_gate(0, 0)
            raise_gate(0, 1)
            each_out(act, measure_out)

        @block.vector
        def _(dve):
            dve.memset(flag_a[:, :], 0.0).then_inc(flag_step, 1)
            dve.wait_ge(flag_step, 1)
            dve.wait_ge(mask_loaded, 16)
            dve.tensor_reduce(flag_a[0:B, 0:1], mask_any[:, :], AX_X, ALU.max).then_inc(flag_step, 1)
            dve.wait_ge(flag_step, 2)
            dve.transpose(flag_b[:, :], flag_a[:, :]).then_inc(flag_step, 1)
            dve.wait_ge(flag_step, 3)
            dve.tensor_reduce(flag[0:1, 0:1], flag_b[0:1, :], AX_X, ALU.max).then_inc(flag_set, 1)

            def statistics(g, b):
                if isinstance(g, int) and g == 0:
                    dve.wait_ge(x_first_loaded, 16)
                else:
                    dve.wait_ge(x_rest_loaded, 16)
                dve.bn_stats(st[:, b, :], x[:, bass.ds(GB * g + b, 1), :].rearrange("p a n -> p (a n)")
                             ).then_inc(st_made, 1)
                wait_apart("dve", dve, st_made, GB * g + b + 1)
                dve.bn_aggr(mv[:, b, :], st[:, b, :]).then_inc(mv_made, 1)

            def variance(g):
                dve.wait_ge(mv_made, GB * g + GB)
                dve.tensor_scalar(vr[:, :].unsqueeze(2), mv[:, :, 1:2],
                                  1.0 + EPS_IN, EPS_LN * EPS_IN, ALU.mult, ALU.add).then_inc(var_ready, 1)

            def normalise(g, b):
                if b >= 2:
                    dve.wait_ge(xt_done, GB * g + b - 1)
                if b == 0:
                    dve.wait_ge(rstd_ready, g + 1)
                i = GB * g + b
                dve.tensor_scalar(normed[:, b % 2, :], x[:, bass.ds(i, 1), :].rearrange("p a n -> p (a n)"),
                                  mv[:, b, 0:1], rstd[:, b:b + 1],
                                  ALU.subtract, ALU.mult).then_inc(norm_ready, 1)

            def keep_x(g, b):
                dve.wait_ge(xt_high, GB * g + b + 1)
                cols = slice(b * L, (b + 1) * L)
                dve.tensor_tensor(x_l[:, :, cols], ps_tr[:, 0:GL].rearrange("p (k n) -> p k n", k=KD),
                                  x_h[:, :, cols].bitcast(F32), ALU.subtract).then_inc(xt_kept, 1)

            def split_low(name, k):
                raw, high, low, scaled = split[name]
                dve.wait_ge(high_made[name], k + 1)
                if scaled:
                    c = dve.scalar_tensor_tensor(out=low[:, k, :], in0=raw[:, k, :], scalar=norm_w[:, k:k + 1],
                                                 in1=high[:, k, :].bitcast(F32), op0=ALU.mult, op1=ALU.subtract)
                else:
                    c = dve.tensor_tensor(low[:, k, :], raw[:, k, :], high[:, k, :].bitcast(F32), ALU.subtract)
                c.then_inc(low_made[name], 1)

            def split_wq(k):
                raw, high, _, _ = split["wq"]
                dve.wait_ge(w_loaded["wq"], 16)
                dve.wait_ge(const_loaded, 32)
                dve.tensor_scalar(high[:, k, :], raw[:, k, :], norm_w[:, k:k + 1], None, ALU.mult
                                  ).then_inc(high_made["wq"], 1)
                split_low("wq", k)

            def keep_mixed_low(geo, g, lot, u):
                dve.wait_ge(mix_high, geo.group_units * g + geo.units * lot + u + 1)
                b = geo.batch(lot, u)
                dst, src = mixed_view(geo, u, b, att_l)
                dve.tensor_tensor(dst, src, mixed_view(geo, u, b, att_h)[0].bitcast(F32), ALU.subtract
                                  ).then_inc(mix_kept, 1)

            def turn_group(g):
                for b in range(GB):
                    normalise(g, b)
                    if b >= 1:
                        keep_x(g, b - 1)
                keep_x(g, GB - 1)

            def make_bias(geo):
                n = NG * geo.keys
                dve.wait_ge(const_loaded, 32)
                dve.tensor_copy(batch_row[:, :, :], ident[0:GB, 0:GB].unsqueeze(2).to_broadcast([GB, GB, L])
                                ).then_inc(picks_made, 1)
                dve.wait_ge(mask_row_loaded, 16)
                dve.tensor_scalar(mask_bias[:, 0:n], mask_row[:, 0:n], -MASKED, MASKED, ALU.mult,
                                  ALU.add).then_inc(bias_made, 1)

            def scores_view(geo):
                return ps_s[0:L, :, 0:geo.bank_heads * geo.keys].rearrange("p k (h n) -> p k h n", h=geo.bank_heads)

            def probs_view(geo, u):
                return probs[u % 2][:, 0:geo.unit_heads * geo.keys].rearrange(
                    "p (k h n) -> p k h n", k=2, h=geo.bank_heads)

            def per_head(t, geo, u):
                return t[:, u % 2, 0:geo.unit_heads]

            def subtract_max(geo, g, lot, u):
                unit = geo.group_units * g + geo.units * lot + u
                dve.wait_ge(scored, unit + 1)
                if u >= 2 or lot:
                    dve.wait_ge(weighted, unit - 1)
                mx = per_head(row_max, geo, u)
                mx4 = mx.rearrange("p (k h) -> p k h", k=2)
                dve.tensor_reduce(mx4, scores_view(geo), AX_X, ALU.max).then_inc(maxed, 1)
                dve.wait_ge(maxed, unit + 1)
                if u >= 2 or lot:
                    dve.wait_ge(turned, unit - 1)
                dve.tensor_tensor(probs_view(geo, u), scores_view(geo),
                                  mx4.unsqueeze(3).to_broadcast([L, 2, geo.bank_heads, geo.keys]),
                                  ALU.subtract).then_inc(shifted, 1)

            def invert_sum(geo, g, lot, u):
                unit = geo.group_units * g + geo.units * lot + u
                dve.wait_ge(raised, unit + 1)
                sm, inv, mx = (per_head(t, geo, u) for t in (row_sum, row_inv, row_max))
                dve.tensor_reduce(sm.rearrange("p (k h) -> p k h", k=2), probs_view(geo, u), AX_X,
                                  ALU.add).then_inc(summed, 1)
                dve.wait_ge(summed, unit + 1)
                dve.reciprocal(inv, sm).then_inc(inverted, 1)
                dve.wait_ge(inverted, unit + 1)
                dve.scalar_tensor_tensor(out=inv, in0=mx, scalar=ALIVE, in1=inv, op0=ALU.is_gt,
                                         op1=ALU.mult).then_inc(weighted, 1)

            def gate_output(g, m):
                dve.wait_ge(done["o"], KD * g + m + 1)
                if m == 0:
                    dve.wait_ge(kept["g"], KD * g + KD)
                dve.scalar_tensor_tensor(out=gate_t[:, m, :], in0=gate_t[:, m, :], scalar=1.0,
                                         in1=ps_mm[m % 2][:, 0:GL], op0=ALU.add, op1=ALU.mult).then_inc(kept["o"], 1)

            def add_to_x(g, b, bank):
                i = GB * g + b
                dve.wait_ge(back1_done, i + 1)
                row = x[:, bass.ds(i, 1), :].rearrange("p a n -> p (a n)")
                dve.scalar_tensor_tensor(out=row, in0=bank[0:L, :], scalar=0.5, in1=row, op0=ALU.mult,
                                         op1=ALU.add).then_inc(x1_ready, 1)

            def statistics1(g, b):
                i = GB * g + b
                row = x[:, bass.ds(i, 1), :].rearrange("p a n -> p (a n)")
                wait_apart("dve", dve, x1_ready, i + 1)
                dve.bn_stats(st1[:, b, :], row).then_inc(st1_made, 1)
                wait_apart("dve", dve, st1_made, i + 1)
                dve.bn_aggr(mv1[:, b, :], st1[:, b, :]).then_inc(mv1_made, 1)
                if b == GB - 1:
                    dve.wait_ge(mv1_made, i + 1)
                    dve.tensor_copy(mean1[:, bass.ds(GB * g, GB)].unsqueeze(2), mv1[:, :, 0:1]
                                    ).then_inc(mean1_ready, 1)
                    dve.tensor_scalar(vr1[:, bass.ds(GB * g, GB)].unsqueeze(2), mv1[:, :, 1:2],
                                      EPS_LN, None, ALU.add).then_inc(var1_ready, 1)

            def normalise2(s, b):
                if b >= 2:
                    dve.wait_ge(tr2_done, GB * s + b - 1)
                if b == 0:
                    dve.wait_ge(rstd1_ready, s + 1)
                i = GB * s + b
                dve.tensor_scalar(normed[:, b % 2, :], x[:, bass.ds(i, 1), :].rearrange("p a n -> p (a n)"),
                                  mean1[:, bass.ds(i, 1)], rstd1[:, bass.ds(i, 1)],
                                  ALU.subtract, ALU.mult).then_inc(norm2_ready, 1)

            def keep_x2_low(s, b):
                dve.wait_ge(tr2_high, GB * s + b + 1)
                cols = slice(b * L, (b + 1) * L)
                high, low = x2_parts(s)
                dve.tensor_tensor(low[:, :, cols], x2_bank(s, b)[:, 0:GL].rearrange("p (k n) -> p k n", k=KD),
                                  high[:, :, cols].bitcast(F32), ALU.subtract).then_inc(tr2_used, 1)

            for b in range(GB):
                statistics(0, b)
            variance(0)

            def tail_part():
                normalise(0, 0)
                normalise(0, 1)
                split_wq(0)
                keep_x(0, 0)
                normalise(0, 2)
                split_wq(1)
                keep_x(0, 1)
                normalise(0, 3)
                split_wq(2)
                keep_x(0, 2)
                split_wq(3)
                keep_x(0, 3)
                for k in range(KD):
                    split_low("wv", k)
                make_bias(tail)

                def body(g, last):
                    n = g + 1
                    for u in range(tail.units):
                        subtract_max(tail, g, 0, u)
                        if u >= 3:
                            keep_mixed_low(tail, g, 0, u - 3)
                        if u >= 1:
                            invert_sum(tail, g, 0, u - 1)
                        if is_first(g):
                            for name, k in first_splits(u):
                                split_low(name, k)
                        if last and u >= GB:
                            keep_x2_low(0, u - GB)
                        if u < GB:
                            if not last:
                                statistics(n, u)
                            if not is_first(g):
                                add_to_x(g - 1, u, ps_tr)
                            if not is_first(g):
                                statistics1(g - 1, u)
                        if u == GB and not last:
                            variance(n)
                        if last and u >= GB - 1:
                            normalise2((u - GB + 1) // GB, (u - GB + 1) % GB)
                        if not last and u >= tail.units - 2:
                            normalise(n, u - tail.units + 2)
                    keep_mixed_low(tail, g, 0, 5)
                    if last:
                        normalise2(1, 1)
                        invert_sum(tail, g, 0, 7)
                        keep_x2_low(1, 0)
                        keep_mixed_low(tail, g, 0, 6)
                        normalise2(1, 2)
                        keep_x2_low(1, 1)
                        normalise2(1, 3)
                        keep_x2_low(1, 2)
                        keep_mixed_low(tail, g, 0, 7)
                        keep_x2_low(1, 3)
                    else:
                        keep_x(n, 0)
                        invert_sum(tail, g, 0, 7)
                        normalise(n, 2)
                        keep_x(n, 1)
                        keep_mixed_low(tail, g, 0, 6)
                        normalise(n, 3)
                        keep_x(n, 2)
                        keep_x(n, 3)
                        keep_mixed_low(tail, g, 0, 7)
                    for m in range(KD):
                        gate_output(g, m)
                    if last:
                        for b, bank in enumerate((ps_tr, ps_pt[:, 0, :], ps_pt[:, 1, :], ps_s[:, 0, :])):
                            add_to_x(g, b, bank)

                each_group(dve, body)

            def full_part():
                make_bias(full)
                for k in range(KD):
                    split_wq(k)
                for name in ("wv", "wg", "wo"):
                    for k in range(KD):
                        split_low(name, k)

                def body(g, last):
                    turn_group(g)
                    for lot in range(GB):
                        for u in range(full.units):
                            subtract_max(full, g, lot, u)
                            if u >= 3:
                                keep_mixed_low(full, g, lot, u - 3)
                            if u >= 1:
                                invert_sum(full, g, lot, u - 1)
                        keep_mixed_low(full, g, lot, 5)
                        invert_sum(full, g, lot, 7)
                        keep_mixed_low(full, g, lot, 6)
                        keep_mixed_low(full, g, lot, 7)
                    for m in range(KD):
                        gate_output(g, m)
                    for b in range(GB):
                        add_to_x(g, b, ps_tr)
                        if not last:
                            statistics1(g, b)
                    if not last:
                        for b in range(GB):
                            statistics(g + 1, b)
                        variance(g + 1)

                each_group(dve, body)
                for s in range(2):
                    for b in range(GB):
                        normalise2(s, b)
                        keep_x2_low(s, b)

            branch(dve, tail_part, full_part)

            def measure(src, i, scale, eps):
                dve.bn_stats(th_st[:, :], src).then_inc(th_st_made, 1)
                wait_apart("dve", dve, th_st_made, i + 1)
                dve.bn_aggr(th_mv[:, :], th_st[:, :]).then_inc(th_mv_made, 1)
                dve.wait_ge(th_mv_made, i + 1)
                dve.tensor_scalar(th_var[:, :], th_mv[:, 1:2], scale, eps, ALU.mult, ALU.add).then_inc(th_var_ready, 1)

            def normalise_thought(src, i):
                dve.wait_ge(th_rstd_ready, i + 1)
                dve.tensor_scalar(th_norm, src, th_mv[:, 0:1], th_rstd[:, 0:1], ALU.subtract,
                                  ALU.mult).then_inc(th_normed, 1)

            def keep_thought(i):
                dve.wait_ge(th_ready, i + 1)
                dve.tensor_copy(thought, ps_pv[0:B, :]).then_inc(th_kept, 1)

            def scale_thought(i, gamma, beta):
                dve.wait_ge(tht_done, i + 1)
                dve.tensor_tensor(th_t0[:, :, :], ps_pt[:, 1, 0:KD * B].rearrange("p (k n) -> p k n", k=KD),
                                  gamma.unsqueeze(2).to_broadcast([P, KD, B]), ALU.mult).then_inc(tht_scaled, 1)
                dve.wait_ge(tht_scaled, i + 1)
                dve.tensor_tensor(th_t[:, :, 0:B], th_t0[:, :, :], beta.unsqueeze(2).to_broadcast([P, KD, B]),
                                  ALU.add).then_inc(tht_ready, 1)

            dve.wait_ge(last_row_loaded, 16)
            measure(last_row, 0, 1.0 + EPS_IN, EPS_LN * EPS_IN)
            normalise_thought(last_row, 0)
            dve.wait_ge(hid_zeroed, 2)
            dve.wait_ge(row_loaded, 16 * 3)
            scale_thought(0, in_gamma, in_beta)
            for b in range(GB):
                statistics1(NG - 1, b)

            def think(s, n, half):
                wait_apart("dve", dve, th_ready, s + 1)
                measure(ps_pv[0:B, :], s + 1, 1.0, EPS_IN)
                normalise_thought(ps_pv[0:B, :], s + 1)
                keep_thought(s)
                if half == 0:
                    normalise2(n, 0)
                scale_thought(s + 1, pn_gamma, pn_beta)
                if half == 0:
                    normalise2(n, 1)
                    keep_x2_low(n, 0)
                    normalise2(n, 2)
                dve.wait_ge(upt_done, s + 1)
                dve.tensor_tensor(z_t.rearrange("p (i j b) -> p i j b", i=KD, j=FJ),
                                  ps_pt[:, 0, :].rearrange("p (i j b) -> p i j b", i=KD, j=FJ)[:, :, :, 0:B],
                                  d1b[:, :, :].unsqueeze(3).to_broadcast([P, KD, FJ, B]), ALU.add).then_inc(z_ready, 1)
                if half == 0:
                    keep_x2_low(n, 1)
                    normalise2(n, 3)
                    keep_x2_low(n, 2)
                    keep_x2_low(n, 3)

            with dve.Fori(0, STEPS // 2) as i:
                for half in range(2):
                    think(2 * i + half, i + 2, half)
            keep_thought(STEPS)
            dve.wait_ge(tht_done, STEPS + 2)
            dve.tensor_copy(th_t[:, :, 0:B], ps_pt[:, 1, 0:KD * B].rearrange("p (k n) -> p k n", k=KD)
                            ).then_inc(tht_ready, 1)
            dve.wait_ge(bc_done, 1)
            for m in range(KD):
                dve.tensor_scalar(bc_half[:, m, :], ps_pv[:, m * B:(m + 1) * B], bc_b[:, m:m + 1], 0.5, ALU.add,
                                  ALU.mult).then_inc(bc_ready, 1)
            dve.wait_ge(bc_ready, KD)
            dve.wait_ge(kept["fg"], KD * NG)

            def finish(g, s):
                i = GB * g + s
                dve.wait_ge(o_rstd_ready, i + 1)
                dve.wait_ge(o_scaled, i + 1)
                dve.scalar_tensor_tensor(out=final[:, s, :], in0=final[:, s, :], scalar=o_rstd[:, s:s + 1],
                                         in1=x[:, bass.ds(i, 1), :].rearrange("p a n -> p (a n)"), op0=ALU.mult,
                                         op1=ALU.add).then_inc(out_ready, 1)

            def output(g, s):
                i = GB * g + s
                dve.wait_ge(back_done, i + 1)
                dve.scalar_tensor_tensor(out=mixed[:, s, :], in0=x[:, bass.ds(i, 1), :].rearrange("p a n -> p (a n)"),
                                         scalar=rstd1[:, bass.ds(i, 1)], in1=back_bank[s][0:L, :], op0=ALU.mult,
                                         op1=ALU.add, accum_out=o_sum[:, s:s + 1]).then_inc(o_ready, 1)
                if not (is_first(g) and s < 2):
                    finish(g if s >= 2 else g - 1, (s - 2) % GB)
                dve.wait_ge(o_ready, i + 1)
                dve.tensor_scalar(o_minus[:, s:s + 1], o_sum[:, s:s + 1], -1.0 / D, None, ALU.mult
                                  ).then_inc(o_minus_ready, 1)
                if not is_first(g):
                    dve.wait_ge(stored[s], 16 * g)
                dve.wait_ge(o_minus_ready, i + 1)
                dve.scalar_tensor_tensor(out=final[:, s, :], in0=mixed[:, s, :], scalar=o_minus[:, s:s + 1],
                                         in1=gamma_row[:, :], op0=ALU.add, op1=ALU.mult).then_inc(o_scaled, 1)

            dve.wait_ge(out_row_loaded, 32)
            each_out(dve, output)
            finish(NG - 1, GB - 2)
            finish(NG - 1, GB - 1)

        @block.gpsimd
        def _(pool):
            for dst, v in ((ones, 1.0), (minus_half, -0.5)):
                pool.memset(dst[:], v).then_inc(filled, 1)
            pool.wait_ge(filled, 2)

            def split_ctx_low(geo, i, c):
                pool.wait_ge(ctx_high_made, geo.v_tiles * i + c + 1)
                raw, rows = ctx_tile(geo, c)
                pool.tensor_tensor(ctx_l[c % 2][:, :, 0:rows], raw, ctx_h[c % 2][:, :, 0:rows].bitcast(F32),
                                   ALU.subtract).then_inc(ctx_low_made, 1)

            def split_fg_low(k):
                raw, high, low, _ = split["fg"]
                pool.wait_ge(high_made["fg"], k + 1)
                pool.tensor_tensor(low[:, k, :], raw[:, k, :], high[:, k, :].bitcast(F32), ALU.subtract
                                   ).then_inc(low_made["fg"], 1)

            def rstd_of(g):
                pool.wait_ge(var_ready, g + 1)
                pool.tensor_tensor(rstd[:, :], vr[:, :], minus_half[:, 0:GB], ALU.pow).then_inc(rstd_ready, 1)

            def rstd1_of(g):
                pool.wait_ge(var1_ready, g + 1)
                pool.tensor_tensor(rstd1[:, bass.ds(GB * g, GB)], vr1[:, bass.ds(GB * g, GB)], minus_half[:, 0:GB],
                                   ALU.pow).then_inc(rstd1_ready, 1)

            def divide(geo, g, lot, u):
                unit = geo.group_units * g + geo.units * lot + u
                pool.wait_ge(weighted, unit + 1)
                w = probs[u % 2][:, 0:geo.unit_heads * geo.keys].rearrange("p (h n) -> p h n", h=geo.unit_heads)
                inv = row_inv[:, u % 2, 0:geo.unit_heads].unsqueeze(2).to_broadcast([L, geo.unit_heads, geo.keys])
                pool.tensor_tensor(w, w, inv, ALU.mult).then_inc(divided, 1)

            pool.memset(keys, 0.0).then_inc(zeroed, 1)
            rstd_of(0)
            pool.wait_ge(const_loaded, 32)
            pool.tensor_scalar(half_gate_b[:, :], gate_b, 0.5, None, ALU.mult).then_inc(half_made, 1)

            def tail_part():
                split_ctx_low(tail, 0, 0)
                split_ctx_low(tail, 0, 1)

                def body(g, last):
                    for u in range(tail.units):
                        if u == GB + 1 and not last:
                            rstd_of(g + 1)
                        if u < 2:
                            split_ctx_low(tail, g, u + 2)
                        divide(tail, g, 0, u)
                        if u == GB - 1 and not is_first(g):
                            rstd1_of(g - 1)
                        if last:
                            for k in fg_splits(u + 1):
                                split_fg_low(k)
                    if not last:
                        split_ctx_low(tail, g + 1, 0)
                        split_ctx_low(tail, g + 1, 1)

                each_group(pool, body)
                pool.wait_ge(turned, tail.group_units * NG)

            def full_part():
                def body(g, last):
                    for lot in range(GB):
                        for c in range(full.v_tiles):
                            split_ctx_low(full, GB * g + lot, c)
                        for u in range(full.units):
                            divide(full, g, lot, u)
                    if not last:
                        rstd1_of(g)
                        rstd_of(g + 1)

                each_group(pool, body)
                pool.wait_ge(turned, full.group_units * NG)
                for k in range(KD):
                    split_fg_low(k)

            branch(pool, tail_part, full_part)
            for dst in (th_t, hid_t):
                pool.memset(dst, 0.0).then_inc(hid_zeroed, 1)

            def thought_rstd(i):
                pool.wait_ge(th_var_ready, i + 1)
                pool.tensor_tensor(th_rstd[:, :], th_var[:, :], minus_half[0:B, 0:1], ALU.pow).then_inc(th_rstd_ready, 1)

            thought_rstd(0)
            rstd1_of(NG - 1)
            with pool.Fori(0, STEPS) as s:
                thought_rstd(s + 1)
            pool.wait_ge(out_row_loaded, 32)

            def out_stage(g, s):
                i = GB * g + s
                row = x[:, bass.ds(i, 1), :].rearrange("p a n -> p (a n)")
                wait_apart("pool", pool, o_ready, i + 1)
                pool.tensor_tensor(row, row, beta_row[:, :], ALU.add).then_inc(x_biased, 1)
                wait_apart("pool", pool, o_squares_ready, i + 1)
                pool.tensor_scalar(o_var[:, s:s + 1], o_squares[:, s:s + 1], 1.0 / D, EPS_IN, ALU.mult, ALU.add
                                   ).then_inc(o_var_ready, 1)
                pool.wait_ge(o_var_ready, i + 1)
                pool.tensor_tensor(o_rstd[:, s:s + 1], o_var[:, s:s + 1], minus_half[:, 0:1],
                                   ALU.pow).then_inc(o_rstd_ready, 1)

            each_out(pool, out_stage)


def kernel(**inputs):
    import numpy as np
    import concourse.bacc as bacc
    from concourse.bass_utils import run_bass_kernel_spmd

    def arr(name):
        return np.asarray(inputs[name])

    def sliced(w):
        return w.reshape(-1, P, w.shape[-1]).transpose(1, 0, 2)

    def per_partition(v):
        return v.reshape(-1, P).T

    def grouped(m):
        return m.reshape(NG, GB, -1).transpose(1, 0, 2).reshape(GB, -1)

    ffn = "L0_ffn_"
    ctx, mask = arr("ctx_2048"), arr("mask_BxS2_bk0")
    ctx_t = ctx.transpose(2, 0, 1).reshape(KD, P, B, M)
    last = ctx_t[:, :, :, HEAD_ROWS:].reshape(KD, P, NG, GB, TAIL)
    arrays = {
        "x": arr("x"),
        "ctx_tail": last.transpose(2, 1, 0, 3, 4).reshape(NG, P, KD * GB * TAIL),
        "ctx_full": ctx_t.transpose(2, 1, 0, 3).reshape(B, P, KD * M),
        "mask": mask,
        "mask_row_tail": grouped(mask[:, HEAD_ROWS:]),
        "mask_row_full": grouped(mask),
        "wq": sliced(arr("L0_xattn_wq").T), "wk": sliced(arr("L0_xattn_wk").T),
        "wv": sliced(arr("L0_xattn_wv").T), "wo": sliced(arr("L0_xattn_wo").T),
        "wg": sliced(arr("L0_xattn_wg").T), "fg": sliced(arr(ffn + "gate_w")),
        "agg": sliced(arr(ffn + "agg_w")), "bc": sliced(arr(ffn + "bc_w")),
        "d1": sliced(arr(ffn + "d1_w")), "d2": sliced(arr(ffn + "d2_w")),
        "vecs": np.stack([per_partition(arr(n)) for n in (
            "L0_xattn_norm_w", ffn + "in_gamma", ffn + "in_beta", ffn + "gate_b", ffn + "bc_b")], axis=1),
        "pn_vecs": np.stack([per_partition(arr(ffn + n)) for n in ("pn_gamma", "pn_beta")], axis=1),
        "d1b": arr(ffn + "d1_b").reshape(FJ, KD, P).transpose(2, 1, 0),
        "agg_b": arr(ffn + "agg_b")[None], "d2_b": arr(ffn + "d2_b")[None],
        "out_gamma": arr(ffn + "out_gamma")[None], "out_beta": arr(ffn + "out_beta")[None],
        "ident": np.eye(P, dtype=np.float32),
        "pick": np.array([[float(r % 32 == b) for b in range(B)] for r in range(P)], np.float32),
    }
    nc = bacc.Bacc("TRN2", target_bir_lowering=False, num_devices=1)
    feeds, a = {}, {}
    for name, v in arrays.items():
        v = np.ascontiguousarray(v)
        feeds[f"in_{name}"] = v
        a[name] = nc.dram_tensor(f"in_{name}", v.shape, mybir.dt.from_np(v.dtype), kind="ExternalInput").ap()
    a["out"] = nc.dram_tensor("out_0", (B, L, D), F32, kind="ExternalOutput").ap()
    xattn_ffn(nc, a)
    r = run_bass_kernel_spmd(nc, [feeds], core_ids=[0])
    return r.results[0]["out_0"]
```
